# Optimizing a Trainium2 kernel written in Bass

```python
import numpy as np
import jax
import jax.numpy as jnp

def _softmax(x, axis=-1):
    return jax.nn.softmax(x, axis=axis)

def _gelu(x):
    return jax.nn.gelu(x, approximate=True)

def _silu(x):
    return jax.nn.silu(x)

def _sigmoid(x):
    return jax.nn.sigmoid(x)

def _layernorm(x, axis=-1, eps=1e-05):
    m = jnp.mean(x, axis=axis, keepdims=True)
    v = jnp.var(x, axis=axis, keepdims=True)
    return (x - m) / jnp.sqrt(v + eps)

def _scatter_add(tgt, idx, src, axis=0):
    return tgt.at[idx].add(src)

def _segment_sum(src, seg, n):
    return jax.ops.segment_sum(src, seg, n)
kernel_name = 'mk_cond_seq_d2_seqx_r4_d72e26'

def setup_inputs(seed: int=0):
    np.random.seed(seed)
    _w = jnp.asarray

    def _rec_inputs():
        import jax
        import jax.numpy as jnp
        _rk = jax.random.key(seed)
        x = 7.22e-05 + 1 * jax.random.normal(jax.random.fold_in(_rk, 1), (32, 256, 256), jnp.float32)
        _lenS = 256 - jax.random.randint(jax.random.fold_in(_rk, 7), (32,), 0, max(1, 256 // 4) + 1, jnp.int32)
        _lenS2 = 256 - jax.random.randint(jax.random.fold_in(_rk, 8), (32,), 0, max(1, 256 // 4) + 1, jnp.int32)
        cond_2048 = 0.00386106 + 1.00199 * jax.random.normal(jax.random.fold_in(_rk, 11), (32, 512), jnp.float32)
        _validS = jnp.arange(256)[None, :] < _lenS[:, None]
        _validS2 = jnp.arange(256)[None, :] < _lenS2[:, None]
        _causal = jnp.tril(jnp.ones((256, 256), dtype=bool))
        mask_BxS_ff1 = jnp.where(jnp.ones((32, 256), dtype=bool), 1.0, 0.0).astype(jnp.float32)
        mask_BxS_ik0 = jnp.where(jnp.broadcast_to(_validS[:, :], (32, 256)), 0, 1).astype(jnp.int32)
        return (x, cond_2048, mask_BxS_ff1, mask_BxS_ik0)
    x, cond_2048, mask_BxS_ff1, mask_BxS_ik0 = _rec_inputs()

    def _L0_cond_setup():
        import jax, jax.numpy as jnp
        import numpy as np
        B, T, D, H, TE = (8, 256, 256, 16, 512)
        LN_EPS = 1e-05

        def layer_norm(x, w, b):
            m = jnp.mean(x, axis=-1, keepdims=True)
            v = jnp.var(x, axis=-1, keepdims=True)
            return (x - m) / jnp.sqrt(v + LN_EPS) * w + b
        key = jax.random.key(seed)
        ks = jax.random.split(key, 8)
        s = lambda k, sh: jax.random.normal(k, sh, jnp.float32) * 0.02
        return dict(x=jax.random.normal(ks[0], (B, T, D), jnp.float32), emb=jax.random.normal(ks[1], (B, TE), jnp.float32), src_mask=jnp.ones((B, T), jnp.float32), norm_w=jnp.ones((D,), jnp.float32), norm_b=jnp.zeros((D,), jnp.float32), q_w=s(ks[2], (D, D)), q_b=jnp.zeros((D,), jnp.float32), k_w=s(ks[3], (D, D)), k_b=jnp.zeros((D,), jnp.float32), v_w=s(ks[4], (D, D)), v_b=jnp.zeros((D,), jnp.float32), emb_w=s(ks[5], (TE, 2 * D)), emb_b=jnp.zeros((2 * D,), jnp.float32), sb_norm_w=jnp.ones((D,), jnp.float32), sb_norm_b=jnp.zeros((D,), jnp.float32), out_w=s(ks[6], (D, D)), out_b=jnp.zeros((D,), jnp.float32))
    _L0_cond_all = _L0_cond_setup()
    _L0_cond_in = {k: v for k, v in _L0_cond_all.items() if k in ('norm_w', 'norm_b', 'q_w', 'q_b', 'k_w', 'k_b', 'v_w', 'v_b', 'emb_w', 'emb_b', 'sb_norm_w', 'sb_norm_b', 'out_w', 'out_b')}
    del _L0_cond_all

    def _L1_cond_setup():
        import jax, jax.numpy as jnp
        import numpy as np
        H = 16
        LN_EPS = 1e-05

        def _layernorm(x, scale, bias):
            mu = jnp.mean(x, axis=-1, keepdims=True)
            var = jnp.var(x, axis=-1, keepdims=True)
            return (x - mu) * jax.lax.rsqrt(var + LN_EPS) * scale + bias
        key = jax.random.key(seed)
        ks = jax.random.split(key, 8)
        B, T, D, E = (4, 1024, 256, 512)
        s = 0.02
        return {'x': jax.random.normal(ks[0], (B, T, D), jnp.float32), 'emb': jax.random.normal(ks[1], (B, E), jnp.float32), 'src_mask': jax.random.randint(ks[2], (B, T), 0, 2).astype(jnp.int32), 'norm_scale': jnp.ones((D,), jnp.float32), 'norm_bias': jnp.zeros((D,), jnp.float32), 'Wq': jax.random.normal(ks[3], (D, D), jnp.float32) * s, 'bq': jnp.zeros((D,), jnp.float32), 'Wk': jax.random.normal(ks[4], (D, D), jnp.float32) * s, 'bk': jnp.zeros((D,), jnp.float32), 'Wv': jax.random.normal(ks[5], (D, D), jnp.float32) * s, 'bv': jnp.zeros((D,), jnp.float32), 'film_emb_W': jax.random.normal(ks[6], (E, 2 * D), jnp.float32) * s, 'film_emb_b': jnp.zeros((2 * D,), jnp.float32), 'film_norm_scale': jnp.ones((D,), jnp.float32), 'film_norm_bias': jnp.zeros((D,), jnp.float32), 'film_out_W': jax.random.normal(ks[7], (D, D), jnp.float32) * s, 'film_out_b': jnp.zeros((D,), jnp.float32)}
    _L1_cond_all = _L1_cond_setup()
    _L1_cond_in = {k: v for k, v in _L1_cond_all.items() if k in ('norm_scale', 'norm_bias', 'Wq', 'bq', 'Wk', 'bk', 'Wv', 'bv', 'film_emb_W', 'film_emb_b', 'film_norm_scale', 'film_norm_bias', 'film_out_W', 'film_out_b')}
    del _L1_cond_all
    return {'x': x, 'cond_2048': cond_2048, 'mask_BxS_ff1': mask_BxS_ff1, 'mask_BxS_ik0': mask_BxS_ik0, 'L0_cond_norm_w': _L0_cond_in['norm_w'], 'L0_cond_norm_b': _L0_cond_in['norm_b'], 'L0_cond_q_w': _L0_cond_in['q_w'], 'L0_cond_q_b': _L0_cond_in['q_b'], 'L0_cond_k_w': _L0_cond_in['k_w'], 'L0_cond_k_b': _L0_cond_in['k_b'], 'L0_cond_v_w': _L0_cond_in['v_w'], 'L0_cond_v_b': _L0_cond_in['v_b'], 'L0_cond_emb_w': _L0_cond_in['emb_w'], 'L0_cond_emb_b': _L0_cond_in['emb_b'], 'L0_cond_sb_norm_w': _L0_cond_in['sb_norm_w'], 'L0_cond_sb_norm_b': _L0_cond_in['sb_norm_b'], 'L0_cond_out_w': _L0_cond_in['out_w'], 'L0_cond_out_b': _L0_cond_in['out_b'], 'L1_cond_norm_scale': _L1_cond_in['norm_scale'], 'L1_cond_norm_bias': _L1_cond_in['norm_bias'], 'L1_cond_Wq': _L1_cond_in['Wq'], 'L1_cond_bq': _L1_cond_in['bq'], 'L1_cond_Wk': _L1_cond_in['Wk'], 'L1_cond_bk': _L1_cond_in['bk'], 'L1_cond_Wv': _L1_cond_in['Wv'], 'L1_cond_bv': _L1_cond_in['bv'], 'L1_cond_film_emb_W': _L1_cond_in['film_emb_W'], 'L1_cond_film_emb_b': _L1_cond_in['film_emb_b'], 'L1_cond_film_norm_scale': _L1_cond_in['film_norm_scale'], 'L1_cond_film_norm_bias': _L1_cond_in['film_norm_bias'], 'L1_cond_film_out_W': _L1_cond_in['film_out_W'], 'L1_cond_film_out_b': _L1_cond_in['film_out_b']}

def reference(x, cond_2048, mask_BxS_ff1, mask_BxS_ik0, L0_cond_norm_w, L0_cond_norm_b, L0_cond_q_w, L0_cond_q_b, L0_cond_k_w, L0_cond_k_b, L0_cond_v_w, L0_cond_v_b, L0_cond_emb_w, L0_cond_emb_b, L0_cond_sb_norm_w, L0_cond_sb_norm_b, L0_cond_out_w, L0_cond_out_b, L1_cond_norm_scale, L1_cond_norm_bias, L1_cond_Wq, L1_cond_bq, L1_cond_Wk, L1_cond_bk, L1_cond_Wv, L1_cond_bv, L1_cond_film_emb_W, L1_cond_film_emb_b, L1_cond_film_norm_scale, L1_cond_film_norm_bias, L1_cond_film_out_W, L1_cond_film_out_b):
    import jax
    import jax.numpy as jnp

    def _L0_cond_ref(x, emb, src_mask, norm_w, norm_b, q_w, q_b, k_w, k_b, v_w, v_b, emb_w, emb_b, sb_norm_w, sb_norm_b, out_w, out_b):
        import jax, jax.numpy as jnp
        import numpy as np
        B, T, D, H, TE = (8, 256, 256, 16, 512)
        LN_EPS = 1e-05

        def layer_norm(x, w, b):
            m = jnp.mean(x, axis=-1, keepdims=True)
            v = jnp.var(x, axis=-1, keepdims=True)
            return (x - m) / jnp.sqrt(v + LN_EPS) * w + b
        Bx, Tx, Dx = x.shape
        xn = layer_norm(x, norm_w, norm_b)
        q = (xn @ q_w + q_b).reshape(Bx, Tx, H, -1)
        k = (xn @ k_w + k_b).reshape(Bx, Tx, H, -1)
        att = jnp.einsum('bnhl,bmhl->bnmh', q, k)
        mask = src_mask.reshape(Bx, 1, Tx, 1)
        att = att + (1.0 - mask) * -1000000.0
        att = jax.nn.softmax(att, axis=2)
        v = ((xn @ v_w + v_b) * src_mask[:, :, None]).reshape(Bx, Tx, H, -1)
        y = jnp.einsum('bnmh,bmhl->bnhl', att, v).reshape(Bx, Tx, Dx)
        e = jax.nn.silu(emb) @ emb_w + emb_b
        scale, shift = jnp.split(e[:, None, :], 2, axis=2)
        h = layer_norm(y, sb_norm_w, sb_norm_b) * (1.0 + scale) + shift
        h = jax.nn.silu(h) @ out_w + out_b
        return x + h

    def _L1_cond_ref(x, emb, src_mask, norm_scale, norm_bias, Wq, bq, Wk, bk, Wv, bv, film_emb_W, film_emb_b, film_norm_scale, film_norm_bias, film_out_W, film_out_b):
        import jax, jax.numpy as jnp
        import numpy as np
        H = 16
        LN_EPS = 1e-05

        def _layernorm(x, scale, bias):
            mu = jnp.mean(x, axis=-1, keepdims=True)
            var = jnp.var(x, axis=-1, keepdims=True)
            return (x - mu) * jax.lax.rsqrt(var + LN_EPS) * scale + bias
        B, T, D = x.shape
        dh = D // H
        xn = _layernorm(x, norm_scale, norm_bias)
        q = xn @ Wq + bq
        k = xn @ Wk + bk
        v = xn @ Wv + bv
        mask = (src_mask == 1)[:, :, None]
        k = jnp.where(mask, -jnp.inf, k)
        v = jnp.where(mask, 0.0, v)
        q = q.reshape(B, T, H, dh).transpose(0, 2, 1, 3)
        k = k.reshape(B, T, H, dh).transpose(0, 2, 1, 3)
        v = v.reshape(B, T, H, dh).transpose(0, 2, 1, 3)
        q = jax.nn.softmax(q, axis=-1)
        k = jax.nn.softmax(k, axis=2)
        attn = jnp.einsum('bhse,bhsd->bhed', k, v)
        y = jnp.einsum('bhtd,bhed->bhte', q, attn)
        y = y.transpose(0, 2, 1, 3).reshape(B, T, D)
        emb_out = jax.nn.silu(emb) @ film_emb_W + film_emb_b
        scale, shift = jnp.split(emb_out, 2, axis=-1)
        h = _layernorm(y, film_norm_scale, film_norm_bias) * (1.0 + scale[:, None, :]) + shift[:, None, :]
        h = jax.nn.silu(h) @ film_out_W + film_out_b
        return x + h
    x = _L0_cond_ref(x, cond_2048, mask_BxS_ff1, L0_cond_norm_w, L0_cond_norm_b, L0_cond_q_w, L0_cond_q_b, L0_cond_k_w, L0_cond_k_b, L0_cond_v_w, L0_cond_v_b, L0_cond_emb_w, L0_cond_emb_b, L0_cond_sb_norm_w, L0_cond_sb_norm_b, L0_cond_out_w, L0_cond_out_b)
    x = _L1_cond_ref(x, cond_2048, mask_BxS_ik0, L1_cond_norm_scale, L1_cond_norm_bias, L1_cond_Wq, L1_cond_bq, L1_cond_Wk, L1_cond_bk, L1_cond_Wv, L1_cond_bv, L1_cond_film_emb_W, L1_cond_film_emb_b, L1_cond_film_norm_scale, L1_cond_film_norm_bias, L1_cond_film_out_W, L1_cond_film_out_b)
    return x

_drawn_inputs = setup_inputs


def setup_inputs(seed=0):
    import zlib

    import numpy as np

    out = dict(_drawn_inputs(seed))
    spreads = {'L0_cond_norm_w': (1.0, 0.6),
     'L0_cond_norm_b': (0.0, 0.1),
     'L0_cond_q_b': (0.0, 0.8),
     'L0_cond_k_b': (0.0, 0.8),
     'L0_cond_v_b': (0.0, 0.1),
     'L0_cond_emb_b': (0.0, 0.1),
     'L0_cond_sb_norm_w': (1.0, 0.2),
     'L0_cond_sb_norm_b': (0.0, 0.301),
     'L0_cond_out_b': (0.0, 0.1),
     'L1_cond_norm_scale': (1.0, 0.2),
     'L1_cond_norm_bias': (0.0, 0.1),
     'L1_cond_bq': (0.0, 0.425),
     'L1_cond_bk': (0.0, 0.8),
     'L1_cond_bv': (0.0, 0.1),
     'L1_cond_film_emb_b': (0.0, 0.1),
     'L1_cond_film_norm_scale': (1.0, 0.2),
     'L1_cond_film_norm_bias': (0.0, 0.38),
     'L1_cond_film_out_b': (0.0, 0.1)}
    factors = {'L1_cond_Wk': 2.989}
    for name, (base, spread) in spreads.items():
        noise = np.random.default_rng([zlib.crc32(name.encode()), seed]).standard_normal(out[name].shape)
        drawn = base * np.exp(spread * noise) if base else spread * noise
        out[name] = jnp.asarray(drawn.astype(out[name].dtype))
    for name, factor in factors.items():
        out[name] = (out[name] * factor).astype(out[name].dtype)
    return out
```

```python
from contextlib import ExitStack

import numpy as np

import concourse.bass as bass
from concourse import mybir

F32 = mybir.dt.float32
BF16 = mybir.dt.bfloat16
I32 = mybir.dt.int32
ALU = mybir.AluOpType
ACT = mybir.ActivationFunctionType
AX = mybir.AxisListType

B = 32
T = 256
D = 256
H = 16
DH = 16
E = 512
EPS = 1e-5
NEG = -1.0e30
ONES = 0x3F803F80
KM = 99
KS = 102
QG = (0, 0, 0, 1, 1, 2)
KG = (0, 1, 2, 0, 1, 0)


class Count:

    def __init__(self, sem, per=1):
        self.sem, self.per = sem, per

    def up(self, ins):
        ins.then_inc(self.sem, 1)

    def wait(self, eng, n, k=None):
        if n >= 0:
            eng.wait_ge(self.sem, self.per * n + (self.per if k is None else k))


class Landed:

    def __init__(self, sems, per=1):
        self.sems, self.per = sems, per

    def up(self, ins, n):
        ins.then_inc(self.sems[n % len(self.sems)], 16)

    def wait(self, eng, n):
        if n >= 0:
            eng.wait_ge(self.sems[n % len(self.sems)], 16 * self.per * (n // len(self.sems) + 1))


def bass_cond_seq_kernel(nc, x, cond, mask_f, mask_i, weights, emb, cols, rows, ident_d, diag_d, out):
    qd = nc.dram_tensor("q_parts", (B, 3, D, T), BF16, kind="Internal").ap()
    kd = nc.dram_tensor("k_parts", (B, 3, D, T), BF16, kind="Internal").ap()
    md = nc.dram_tensor("mask_parts", (B, 3, T), BF16, kind="Internal").ap()

    nd = nc.dram_tensor("key_mask", (B, T), F32, kind="Internal").ap()

    with ExitStack() as ctx:
        def sb(name, shape, dt=F32):
            return ctx.enter_context(nc.sbuf_tensor("sb_" + name, shape, dt))

        def sem(name):
            return ctx.enter_context(nc.semaphore(name))

        def count(name, per=1):
            return Count(sem(name), per)

        def landed(name, ring, per=1):
            return Landed([sem(f"{name}{i}") for i in range(ring)], per)

        psT = [ctx.enter_context(nc.psum_tensor(f"psT{i}", [128, 1024], F32)) for i in range(2)]
        psM = [ctx.enter_context(nc.psum_tensor(f"psM{i}", [128, 512], F32)) for i in range(2)]
        psY = ctx.enter_context(nc.psum_tensor("psY", [128, 512], F32))
        psX = ctx.enter_context(nc.psum_tensor("psX", [128, 512], F32))

        Y = sb("Y", [128, max(2 * B, 20), D])
        Wt = [sb(f"W{l}", [128, 4, 2, D]) for l in range(2)]
        W = [[Wt[l][:, n, :, :] for n in range(4)] for l in range(2)]
        EW = Y[:, 0:16, :].rearrange("p (l k a) n -> p l k (a n)", l=2, k=4)
        Qs = [sb(f"Qs{i}", [128, H, T], BF16) for i in range(3)]
        Ks = [sb(f"Ks{i}", [128, H, T], BF16) for i in range(3)]
        P = [sb(f"P{i}", [128, 1024]) for i in range(4)]
        Vp = [sb(f"Vp{i}", [128, 2, H, 32]) for i in range(4)]
        ident = sb("ident", [128, 128])
        xt = [sb(f"xt{i}", [128, 2, D]) for i in range(2)]
        xn = sb("xn", [128, 2, D])
        xT = sb("xT", [128, 2, T])
        qf = [sb(f"qf{i}", [128, 2, T]) for i in range(2)]
        rf = sb("rf", [128, 2, T])
        qp = [sb(f"qp{i}", [128, 3, 2, T], BF16) for i in range(2)]
        vt = sb("vt", [128, 2, D])
        yT = sb("yT", [128, 4, T])
        yr = sb("yr", [128, 2, D])
        rb = sb("rb", [128, 5, D])
        vb0, ob0, qb1, vb1, ob1 = (rb[:, r:r + 1, :].to_broadcast([128, 2, D]) for r in range(5))
        cm = [sb(f"cm{i}", [128, 2 * H]) for i in range(2)]
        cp = [sb(f"cp{i}", [16, 3, 128], BF16) for i in range(2)]
        cr = sb("cr", [16, 128])
        st = sb("st", [128, 4, 6])
        mv = sb("mv", [128, 4, 2])
        ve = sb("ve", [128, 4])
        rs = sb("rs", [128, 4])
        rd = sb("rd", [128, H])
        ph = sb("ph", [128, 2])
        bq = sb("bq", [128, 6])
        col = sb("col", [128, 2, 16])
        cT = sb("cT", [128, 4, B])
        cond_sb = Y[0:B, 16:18, :].rearrange("b a n -> b (a n)")
        tc = Y[:, 18, 0:4 * B].rearrange("p (k b) -> p k b", k=4)
        sc = Y[:, 19, 0:B]
        FA = sb("FA", [128, 2, 2, B])
        FB = sb("FB", [128, 2, 2, B])
        irow = sb("irow", [B, T], I32)
        kT = sb("kT", [128, 2, B])
        mrow = sb("mrow", [B, T])
        mr2 = sb("mr2", [B, T])
        mp = sb("mp", [B, 3, T], BF16)
        mT = sb("mT", [128, 2, B])
        mr3 = sb("mr3", [B, T])
        keep = sb("keep", [B, T])
        diag = sb("diag", [128, 128])
        BD = sb("BD", [128, 4, 136])
        qm = sb("qm", [128, 2 * H])
        kx = sb("kx", [128, 2])
        ksum = sb("ksum", [128, 2])
        kd2 = sb("kd2", [128, 2])

        s_ld = sem("s_ld")
        n_ld = [0]
        s_set = sem("s_set")
        s_x = landed("s_x", 2)
        s_st = count("s_st", 4)
        s_ve = count("s_ve")
        s_rs = count("s_rs")
        s_xn = count("s_xn")
        s_xtr = count("s_xtr")
        s_xT = count("s_xT")
        s_qm = count("s_qm", 2)
        s_qf = count("s_qf", 2)
        s_hi = count("s_hi", 2)
        s_rf = count("s_rf", 2)
        s_mi = count("s_mi", 2)
        s_lo = count("s_lo", 2)
        s_qo = [landed("s_qo", 2), landed("s_ko", 2)]
        s_in = landed("s_in", 3, 13)
        s_vm = count("s_vm")
        s_vt = count("s_vt")
        s_v = count("s_v")
        s_sm = count("s_sm", H)
        s_mx = count("s_mx", H)
        s_ct = count("s_ct", 2)
        s_cs = count("s_cs", 8)
        s_cin = [landed("s_ca", 2, 3), landed("s_cb", 2, 3)]
        s_sT = count("s_sT", 8)
        s_ex = count("s_ex", 8)
        s_pv = count("s_pv", 4)
        s_ye = count("s_ye", 4)
        s_yt = count("s_yt", 2)
        s_yd = count("s_yd", 8)
        s_yv = count("s_yv", 2)
        s_yr = count("s_yr", 2)
        s_y = count("s_y", 2)

        block = ctx.enter_context(nc.Block())
        pre = {}

        def each(fn):
            for t in range(B + 4):
                for i in range(8):
                    fn(t, i)

        def ok(n):
            return 0 <= n < B

        s_p = {k: count("p_" + k) for k in ("ve0", "pe", "act", "pool", "mneg", "film")}
        s_md = landed("s_md", 1, 2)

        room = [r[:, :, :].rearrange("p h t -> p (h t)").bitcast(F32)[:, 512 * u:512 * u + 512]
                for r in Qs + Ks for u in range(4)]
        room += [r[:, 512 * u:512 * u + 512] for r in P for u in range(2)]
        room += [r[:, u, :, :].rearrange("p h d -> p (h d)") for r in Vp for u in range(2)]

        def unit():
            return room.pop(0).rearrange("p (k t) -> p k t", k=2)

        xr = [unit() for _ in range(3)]
        x1 = [unit() for _ in range(9)]
        kr = [unit() for _ in range(2)]
        ub, th, hb = ([unit() for _ in range(2)] for _ in range(3))
        xb, tq, km, ke, ken, kn, v1, yn, ob = (unit() for _ in range(9))
        vk, qe = ([unit() for _ in range(2)] for _ in range(2))
        R = [psT[0][:, 0:512], psT[0][:, 512:1024], psT[1][:, 0:512], psT[1][:, 512:1024],
             psM[0][:, :], psM[1][:, :], psY[:, :], psX[:, :]]

        def tiles(bank):
            return bank.rearrange("p (k t) -> p k t", k=2)

        e_xr = landed("e_xr", 3)
        e_kr = landed("e_kr", 2)
        e_xb = count("e_xb", 2)
        e_f = [count(f"e_f{l}") for l in range(2)]
        e_u = [count(f"e_u{l}") for l in range(2)]
        e_t = [count(f"e_t{l}") for l in range(2)]
        e_h = [count(f"e_h{l}") for l in range(2)]
        e_o = [count(f"e_o{l}") for l in range(2)]
        e_x1 = count("e_x1", 5)
        e_g = [count(f"e_g{l}", 2) for l in range(2)]
        e_xn = count("e_xn")
        e_tr = count("e_tr")
        e_xT = count("e_xT")
        e_q, e_k, e_v = count("e_q"), count("e_k"), count("e_v")
        e_dq = count("e_dq", 2)
        e_dk = count("e_dk", 3)
        e_dv = count("e_dv")
        e_qs = count("e_qs")
        e_vk = count("e_vk")
        e_ke = count("e_ke")
        e_kd = count("e_kd")
        e_kk = count("e_kk")
        e_qt, e_kt = count("e_qt"), count("e_kt")
        e_qe, e_kn = count("e_qe"), count("e_kn")
        e_kv = count("e_kv")
        e_bd = count("e_bd")
        e_y = count("e_y", 2)
        e_yd = count("e_yd", 8)
        e_yn = count("e_yn")
        e_ob = count("e_ob")
        e_out = landed("e_out", 1)

        def rounds(stage):
            for t in range(B + 8):
                for k in range(8, -1, -1):
                    if 0 <= t - k < B:
                        stage(k, t - k)

        def both(ap):
            return ap.to_broadcast([128, 2, D])

        def phase2_sp(sp):
            s_y.wait(sp, B - 1)

            def load(n):
                e_xr.up(sp.dma_start(xr[n % 3], x[n].rearrange("(k p) d -> p k d", p=128)), n)
            load(0)
            load(1)
            for t in range(B + 8):
                if t + 2 < B:
                    e_xb.wait(sp, t - 1, 1)
                    load(t + 2)
                if t >= 2 and t - 2 < B:
                    n = t - 2
                    e_dk.wait(sp, n - 2)
                    e_kr.up(sp.dma_start(kr[n % 2][:, 0, :], nd[n:n + 1, :].to_broadcast([128, T])), n)
                if t >= 8:
                    n = t - 8
                    e_ob.wait(sp, n)
                    e_out.up(sp.dma_start(out[n].rearrange("(k p) d -> p k d", p=128), ob), n)
            e_out.wait(sp, B - 1)

        def phase2_gpsimd(g):
            s_y.wait(g, B - 1)

            def rstd(n, l, done):
                done.wait(g, n)
                e_g[l].up(g.tensor_scalar(ve[:, 2 * l:2 * l + 2], mv[:, 2 * l:2 * l + 2, 1], EPS, None, ALU.add))
                e_g[l].wait(g, n, 1)
                e_g[l].up(g.tensor_tensor(rs[:, 2 * l:2 * l + 2], ve[:, 2 * l:2 * l + 2], ph[:, :], ALU.pow))
                e_g[l].wait(g, n, 2)

            def stage(k, n):
                if k == 0:
                    e_xr.wait(g, n)
                    e_x1.wait(g, n - 1)
                    e_xb.up(g.tensor_tensor(xb, xr[n % 3], ob0, ALU.add))
                if k == 1:
                    rstd(n, 0, e_x1)
                    e_tr.wait(g, n - 1)
                    for i in range(2):
                        ins = g.tensor_scalar(xn[:, i, :], x1[n % 9][:, i, :], mv[:, i, 0:1], rs[:, i:i + 1],
                                              ALU.subtract, ALU.mult)
                    e_xn.up(ins)
                    e_xn.wait(g, n)
                    e_xb.up(g.tensor_tensor(x1[n % 9], x1[n % 9], ob1, ALU.add))
                if k == 3:
                    e_dq.wait(g, n)
                    e_qt.wait(g, n - 1)
                    e_qs.up(g.tensor_tensor(
                        tq.rearrange("p k (h d) -> p (k h) d", d=DH), tq.rearrange("p k (h d) -> p (k h) d", d=DH),
                        qm[:, :].rearrange("p (h a) -> p h a", a=1).to_broadcast([128, 2 * H, DH]), ALU.add))
                    e_dv.wait(g, n)
                    e_kv.wait(g, n - 2)
                    for i in range(2):
                        ins = g.tensor_scalar(vk[n % 2][:, i, :], v1[:, i, :], kT[:, i, n:n + 1], None, ALU.mult)
                    e_vk.up(ins)
                if k == 4:
                    e_kd.wait(g, n)
                    e_kt.wait(g, n - 1)
                    for i in range(2):
                        ins = g.tensor_scalar(ken[:, i, :], ke[:, i, :], kd2[:, i:i + 1], None, ALU.mult)
                    e_kk.up(ins)
                if k == 6:
                    rstd(n, 1, e_yd)
                    e_f[1].wait(g, n - 1)
                    for i in range(2):
                        ins = g.tensor_scalar(yn[:, i, :], yr[:, i, :], mv[:, 2 + i, 0:1], rs[:, 2 + i:3 + i],
                                              ALU.subtract, ALU.mult)
                    e_yn.up(ins)
            rounds(stage)

        def phase2_act(a):
            s_y.wait(a, B - 1)

            def film(n, l):
                e_f[l].wait(a, n)
                e_h[l].wait(a, n - 1)
                for d in range(2):
                    ins = a.activation(ub[l][:, d, :], R[l][:, T * d:T * d + T], ACT.Identity,
                                       bias=FB[:, l, d, n:n + 1], scale=FA[:, l, d, n:n + 1])
                e_u[l].up(ins)
                e_u[l].wait(a, n)
                e_t[l].up(a.activation(th[l], ub[l], ACT.Tanh))

            def stage(k, n):
                if k == 0:
                    film(n, 0)
                if k == 2:
                    e_tr.wait(a, n)
                    e_v.wait(a, n - 1)
                    e_xT.up(a.activation(xT[:, :, :], tiles(R[5]), ACT.Identity))
                if k == 3:
                    e_dk.wait(a, n)
                    e_kk.wait(a, n - 1)
                    for i in range(2):
                        ins = a.activation(ke[:, i, :], km[:, i, :], ACT.Exp, bias=kx[:, i:i + 1],
                                           accum_out=ksum[:, i:i + 1])
                    e_ke.up(ins)
                if k == 4:
                    e_qt.wait(a, n)
                    e_y.wait(a, n - 2)
                    e_qe.up(a.activation(qe[n % 2], tiles(R[2]), ACT.Exp))
                    e_kt.wait(a, n)
                    e_kv.wait(a, n - 1)
                    e_kn.up(a.activation(kn, tiles(R[3]), ACT.Identity))
                if k == 7:
                    film(n, 1)
            rounds(stage)

        def phase2_dve(v):
            s_y.wait(v, B - 1)

            def silu(n, l):
                e_t[l].wait(v, n)
                e_o[l].wait(v, n - 1)
                e_h[l].up(v.scalar_tensor_tensor(hb[l], th[l], 1.0, ub[l], ALU.add, ALU.mult))

            def stage(k, n):
                if k == 0:
                    silu(n, 0)
                if k == 1:
                    e_o[0].wait(v, n)
                    e_xb.wait(v, n, 1)
                    e_ob.wait(v, n - 9)
                    e_x1.up(v.tensor_tensor(x1[n % 9], tiles(R[6]), xb, ALU.add))
                    e_x1.wait(v, n, 1)
                    e_xn.wait(v, n - 1)
                    for i in range(2):
                        e_x1.up(v.bn_stats(st[:, i, :], x1[n % 9][:, i, :]))
                    for i in range(2):
                        e_x1.wait(v, n, 2 + i)
                        e_x1.up(v.bn_aggr(mv[:, i, :], st[:, i, :]))
                if k == 3:
                    e_q.wait(v, n)
                    e_qs.wait(v, n - 1)
                    e_qt.wait(v, n - 1)
                    e_dq.up(v.tensor_tensor(tq, tiles(R[2]), qb1, ALU.add))
                    e_dq.wait(v, n, 1)
                    e_dq.up(v.tensor_reduce(qm[:, :], tq.rearrange("p k (h d) -> p (k h) d", d=DH), AX.X, ALU.max,
                                            negate=True))
                    e_k.wait(v, n)
                    e_kr.wait(v, n)
                    e_ke.wait(v, n - 1)
                    for i in range(2):
                        e_dk.up(v.scalar_tensor_tensor(km[:, i, :], R[3][:, T * i:T * i + T], bq[:, 4 + i:5 + i],
                                                       kr[n % 2][:, 0, :], ALU.add, ALU.add))
                    e_dk.wait(v, n, 2)
                    e_dk.up(v.tensor_reduce(kx[:, :], km, AX.X, ALU.max, negate=True))
                    e_v.wait(v, n)
                    e_vk.wait(v, n - 1)
                    e_dv.up(v.tensor_tensor(v1, tiles(R[4]), vb1, ALU.add))
                    e_ke.wait(v, n)
                    e_kk.wait(v, n - 1)
                    e_kd.up(v.reciprocal(kd2[:, :], ksum[:, :]))
                if k == 5:
                    e_kv.wait(v, n)
                    e_y.wait(v, n - 2)
                    e_bd.up(v.tensor_tensor(BD[:, 2 * (n % 2):2 * (n % 2) + 2, 0:128],
                                            R[4][:, 0:256].rearrange("p (k t) -> p k t", k=2),
                                            diag[:, :].rearrange("p (a e) -> p a e", a=1).to_broadcast([128, 2, 128]),
                                            ALU.mult))
                if k == 6:
                    e_yn.wait(v, n - 1)
                    for i in range(2):
                        e_y.wait(v, n, i + 1)
                        ps = R[(5, 7)[i]][:, 0:272].rearrange("p (k e) -> p k e", k=2)
                        e_yd.up(v.reciprocal(rd[:, 0:H].rearrange("p (k h) -> p k h", k=2), ps[:, :, 128:136]))
                        e_yd.wait(v, n, 4 * i + 1)
                        for f in range(2):
                            ins = v.tensor_tensor(
                                yr[:, i, 128 * f:128 * f + 128].rearrange("p (h e) -> p h e", e=DH),
                                ps[:, f, 0:128].rearrange("p (h e) -> p h e", e=DH),
                                rd[:, 8 * f:8 * f + 8].rearrange("p (h a) -> p h a", a=1).to_broadcast([128, 8, DH]),
                                ALU.mult)
                        e_yd.up(ins)
                        e_yd.wait(v, n, 4 * i + 2)
                        e_yd.up(v.bn_stats(st[:, 2 + i, :], yr[:, i, :]))
                        e_yd.wait(v, n, 4 * i + 3)
                        e_yd.up(v.bn_aggr(mv[:, 2 + i, :], st[:, 2 + i, :]))
                if k == 7:
                    silu(n, 1)
                if k == 8:
                    e_o[1].wait(v, n)
                    e_xb.wait(v, n, 2)
                    e_out.wait(v, n - 1)
                    e_ob.up(v.tensor_tensor(ob, tiles(R[6]), x1[n % 9], ALU.add))
            rounds(stage)

        def phase2_pe(pe):
            s_y.wait(pe, B - 1)
            read = {}

            def take(bank, *by):
                if bank in read:
                    read[bank][0].wait(pe, *read[bank][1:])
                read[bank] = by

            def film(n, l, src):
                take(l, e_u[l], n)
                for d in range(2):
                    for i in range(2):
                        ins = pe.transpose(R[l][:, T * d + 128 * i:T * d + 128 * i + 128],
                                           src[i][:, 128 * d:128 * d + 128], ident[:, :])
                e_f[l].up(ins)

            def natural(bank, lhs, w):
                for i in range(2):
                    for d in range(2):
                        ins = pe.matmul(R[bank][:, T * i:T * i + T], lhs[:, d, 128 * i:128 * i + 128], w[:, d, :],
                                        start=(d == 0), stop=(d == 1))
                return ins

            def stage(k, n):
                if k == 0:
                    film(n, 0, [Y[:, 2 * n + i, :] for i in range(2)])
                if k == 1:
                    e_h[0].wait(pe, n)
                    take(6, e_x1, n, 1)
                    e_o[0].up(natural(6, hb[0], W[0][3]))
                if k == 2:
                    e_xn.wait(pe, n)
                    take(5, e_xT, n)
                    for d in range(2):
                        for i in range(2):
                            ins = pe.transpose(R[5][:, T * d + 128 * i:T * d + 128 * i + 128],
                                               xn[:, i, 128 * d:128 * d + 128], ident[:, :])
                    e_tr.up(ins)
                if k == 3:
                    e_xT.wait(pe, n)
                    take(2, e_dq, n, 1)
                    e_q.up(natural(2, xT, W[1][0]))
                    take(3, e_dk, n, 2)
                    for o in range(2):
                        for d in range(2):
                            ins = pe.matmul(R[3][:, T * o:T * o + T], W[1][1][:, d, 128 * o:128 * o + 128],
                                            xT[:, d, :], start=(d == 0), stop=(d == 1))
                    e_k.up(ins)
                    take(4, e_dv, n)
                    e_v.up(natural(4, xT, W[1][2]))
                if k == 4:
                    e_qs.wait(pe, n)
                    take(2, e_qe, n)
                    for d in range(2):
                        for i in range(2):
                            ins = pe.transpose(R[2][:, T * d + 128 * i:T * d + 128 * i + 128],
                                               tq[:, i, 128 * d:128 * d + 128], ident[:, :])
                    e_qt.up(ins)
                    e_kk.wait(pe, n)
                    take(3, e_kn, n)
                    for i in range(2):
                        for d in range(2):
                            ins = pe.transpose(R[3][:, T * i + 128 * d:T * i + 128 * d + 128],
                                               ken[:, d, 128 * i:128 * i + 128], ident[:, :])
                    e_kt.up(ins)
                if k == 5:
                    e_kn.wait(pe, n)
                    e_vk.wait(pe, n)
                    take(4, e_bd, n)
                    for f in range(2):
                        for i in range(2):
                            ins = pe.matmul(R[4][:, 128 * f:128 * f + 128], vk[n % 2][:, i, 128 * f:128 * f + 128],
                                            kn[:, i, 128 * f:128 * f + 128], start=(i == 0), stop=(i == 1))
                    e_kv.up(ins)
                if k == 6:
                    e_bd.wait(pe, n)
                    e_qe.wait(pe, n)
                    for i in range(2):
                        take((5, 7)[i], e_yd, n, 4 * i + 2)
                        for f in range(2):
                            ins = pe.matmul(R[(5, 7)[i]][:, 136 * f:136 * f + 136], qe[n % 2][:, f, 128 * i:128 * i + 128],
                                            BD[:, 2 * (n % 2) + f, :], start=True, stop=True)
                        e_y.up(ins)
                if k == 7:
                    e_yn.wait(pe, n)
                    film(n, 1, [yn[:, i, :] for i in range(2)])
                if k == 8:
                    e_h[1].wait(pe, n)
                    take(6, e_ob, n)
                    e_o[1].up(natural(6, hb[1], W[1][3]))
            rounds(stage)
        @block.sync
        def _(sp):
            def load(dst, src):
                sp.dma_start(dst, src).then_inc(s_ld, 16)
                n_ld[0] += 16
            load(ident[:, :], ident_d)
            load(mrow[:, :], mask_f)
            load(irow[:, :], mask_i)
            load(Wt[0][:, :, :, :], weights[:, 0])
            load(col[:, :, :], cols)
            load(rb[:, :, :], rows.rearrange("(a r) n -> a r n", a=1).to_broadcast([128, 5, D]))
            load(cond_sb, cond)
            load(EW, emb)
            load(Wt[1][:, :, :, :], weights[:, 1])
            load(diag[:, :], diag_d)
            pre["ld"] = n_ld[0]
            sp.dma_start(xt[0][:, :, :], x[0].rearrange("(k p) d -> p k d", p=128)).then_inc(s_x.sems[0], 16)
            s_p["ve0"].wait(sp, 6)
            s_p["pool"].wait(sp, 0)
            s_md.up(sp.dma_start(md.rearrange("b c t -> b (c t)"), mp[:, :, :]), 0)
            s_p["mneg"].wait(sp, 2)
            s_md.up(sp.dma_start(nd, mr3[:, :]), 0)
            s_md.wait(sp, 0)

            def c_in(n, hf):
                s_cs.wait(sp, n, 4 * hf + 4)
                for p in range(3):
                    s_cin[hf].up(sp.dma_start(
                        Qs[n % 3][KM + p:KM + p + 1, 8 * hf:8 * hf + 8, :], cp[hf][:, p, :]), n)

            def parts(n, w):
                dst, dram, groups = ((Qs, qd, QG), (Ks, kd, KG))[w]
                s_lo.wait(sp, n, w + 1)
                s_qo[w].up(sp.dma_start(dram[n].rearrange("c (o p) t -> p c o t", p=128), qp[w][:, :, :, :]), n)
                s_qo[w].wait(sp, n)
                if w == 0:
                    s_sT.wait(sp, n - 3)
                else:
                    s_in.up(sp.dma_start(Ks[n % 3][96:99, :, :],
                                         md[n].rearrange("c (a t) -> c a t", a=1).to_broadcast([3, H, T])), n)
                for g, part in enumerate(groups):
                    s_in.up(sp.dma_start(dst[n % 3][16 * g:16 * g + 16, :, :],
                                         dram[n, part].rearrange("(h d) t -> d h t", d=DH)), n)

            for t in range(B + 4):
                if ok(t + 1):
                    s_xn.wait(sp, t - 1)
                    s_x.up(sp.dma_start(xt[(t + 1) % 2][:, :, :], x[t + 1].rearrange("(k p) d -> p k d", p=128)), t + 1)
                if ok(t - 3):
                    c_in(t - 3, 1)
                if ok(t - 2):
                    c_in(t - 2, 0)
                if ok(t):
                    parts(t, 0)
                    parts(t, 1)
            phase2_sp(sp)

        @block.gpsimd
        def _(g):
            z = s_p["pool"]
            for i in range(3):
                ins = g.memset(Ks[i][96:KS, :, :].bitcast(I32), ONES)
            z.up(ins)
            z.wait(g, 0)
            g.memset(ph[:, :], -0.5)
            for i in range(4):
                ins = g.memset(Vp[i][:, :, :, 17:32], 0.0)
                ins = g.memset(Vp[i][:, :, :, 16:17], 1.0)
            z.up(ins)
            z.wait(g, 1)

            def slot(t, i):
                if i == 0 and ok(t):
                    s_st.wait(g, t)
                    s_ve.up(g.tensor_scalar(ve[:, 0:2], mv[:, 0:2, 1], EPS, None, ALU.add))
                    s_ve.wait(g, t)
                    s_rs.up(g.tensor_tensor(rs[:, 0:2], ve[:, 0:2], ph[:, :], ALU.pow))
                    s_rs.wait(g, t)
                    s_xtr.wait(g, t - 1)
                    for k in range(2):
                        ins = g.tensor_scalar(xn[:, k, :], xt[t % 2][:, k, :], mv[:, k, 0:1], rs[:, k:k + 1],
                                              ALU.subtract, ALU.mult)
                    s_xn.up(ins)
                if i in (1, 2) and ok(t - 4):
                    n, k = t - 4, i - 1
                    s_yd.wait(g, n, 4 * k + 4)
                    s_yv.up(g.tensor_scalar(ve[:, 2 + k:3 + k], mv[:, 2 + k, 1:2], EPS, None, ALU.add))
                    s_yv.wait(g, n, k + 1)
                    s_yr.up(g.tensor_tensor(rs[:, 2 + k:3 + k], ve[:, 2 + k:3 + k], ph[:, 0:1], ALU.pow))
                    s_yr.wait(g, n, k + 1)
                    s_p["film"].wait(g, 21)
                    s_y.up(g.tensor_scalar(Y[:, 2 * n + k, :], yr[:, k, :], mv[:, 2 + k, 0:1], rs[:, 2 + k:3 + k],
                                           ALU.subtract, ALU.mult))
                if i in (4, 6) and ok(t):
                    w = (i - 4) // 2
                    s_hi.wait(g, t, w + 1)
                    if w == 0:
                        s_lo.wait(g, t - 1)
                    else:
                        s_lo.wait(g, t, 1)
                    s_rf.up(g.tensor_tensor(rf[:, :, :], qf[w][:, :, :], qp[w][:, 0, :, :], ALU.subtract))
                if i in (5, 7) and ok(t):
                    w = (i - 5) // 2
                    s_mi.wait(g, t, w + 1)
                    s_lo.up(g.tensor_tensor(qp[w][:, 2, :, :], rf[:, :, :], qp[w][:, 1, :, :], ALU.subtract))
                if i == 7 and ok(t):
                    s_vt.wait(g, t)
                    s_pv.wait(g, t - 4)
                    for k in range(2):
                        ins = g.tensor_scalar(Vp[t % 4][:, k, :, 0:16],
                                              vt[:, k, :].rearrange("p (h d) -> p h d", d=DH),
                                              mT[:, k, t:t + 1], None, ALU.mult)
                    s_v.up(ins)
            each(slot)
            phase2_gpsimd(g)

        @block.scalar
        def _(a):
            done = s_p["act"]
            s_p["pe"].wait(a, 0)
            for k, dst in enumerate((mT, kT)):
                ins = a.activation(dst[:, :, :], psX[:, 2 * B * k:2 * B * k + 2 * B].rearrange("p (k b) -> p k b", k=2),
                                   ACT.Identity)
            done.up(ins)
            s_p["pe"].wait(a, 1)
            done.up(a.activation(tc, psM[1][:, 0:4 * B].rearrange("p (k b) -> p k b", k=4), ACT.Tanh, scale=0.5))
            s_p["pe"].wait(a, 2)
            for n, (l, w) in enumerate(((0, 0), (0, 1), (1, 1))):
                for o in range(2):
                    ins = a.activation(bq[:, 2 * n + o:2 * n + o + 1], psM[0][:, 2 * n + o:2 * n + o + 1], ACT.Identity,
                                       bias=col[:, l, 4 + 2 * w + o:5 + 2 * w + o])
            done.up(ins)
            done.wait(a, 2)

            def slot(t, i):
                if ok(t - 3):
                    n = t - 3
                    G = 8 * n + i
                    s_sT.wait(a, n, i + 1)
                    if G >= 4:
                        a.wait_ge(s_pv.sem, (G - 4) // 2 + 1)
                    s_ex.up(a.activation(P[G % 4][:, :], psT[G % 2][:, :], ACT.Exp))
                if i % 2 == 0:
                    n, gr = (t - 3, i // 2 - 1) if i else (t - 4, 3)
                    if ok(n):
                        s_pv.wait(a, n, gr + 1)
                        s_yt.wait(a, n - 1)
                        s_ye.up(a.activation(yT[:, gr, :], psY[:, 0:T], ACT.Identity))
                if i == 3 and ok(t):
                    s_xtr.wait(a, t)
                    s_vm.wait(a, t - 1)
                    s_xT.up(a.activation(xT[:, :, :], psX[:, :].rearrange("p (k t) -> p k t", k=2), ACT.Identity))
                if i in (4, 6) and ok(t):
                    w = (i - 4) // 2
                    s_qm.wait(a, t, w + 1)
                    s_rf.wait(a, t - 1, w + 1)
                    for o in range(2):
                        ins = a.activation(qf[w][:, o, :], psX[:, T * o:T * o + T], ACT.Identity,
                                           bias=bq[:, 2 * w + o:2 * w + o + 1])
                    s_qf.up(ins)
            each(slot)
            phase2_act(a)

        @block.vector
        def _(v):
            z = s_p["ve0"]
            for i in range(3):
                ins = v.memset(Qs[i][96:KS, :, :].bitcast(I32), ONES)
            z.up(ins)
            v.wait_ge(s_ld, pre["ld"])
            y = s_p["mneg"]
            y.up(v.tensor_scalar(mr3[:, :], irow[:, :], 1, None, ALU.is_equal))
            y.wait(v, 0)
            y.up(v.tensor_scalar(keep[:, :], mr3[:, :], -1.0, 1.0, ALU.mult, ALU.add))
            y.wait(v, 1)
            y.up(v.tensor_scalar(mr3[:, :], mr3[:, :], NEG, None, ALU.mult))
            z.up(v.tensor_scalar(mr2[:, :], mrow[:, :], -1.0, 1.0, ALU.mult, ALU.add))
            z.wait(v, 1)
            z.up(v.tensor_scalar(mr2[:, :], mr2[:, :], -1000000.0, None, ALU.mult))
            z.wait(v, 2)
            z.up(v.tensor_copy(mp[:, 0, :], mr2[:, :]))
            z.wait(v, 3)
            z.up(v.tensor_tensor(mr2[:, :], mr2[:, :], mp[:, 0, :], ALU.subtract))
            z.wait(v, 4)
            z.up(v.tensor_copy(mp[:, 1, :], mr2[:, :]))
            z.wait(v, 5)
            z.up(v.tensor_tensor(mp[:, 2, :], mr2[:, :], mp[:, 1, :], ALU.subtract))
            y = s_p["film"]
            s_p["act"].wait(v, 1)
            y.up(v.scalar_tensor_tensor(cT[:, :, :], tc, 1.0, psM[1][:, 0:4 * B].rearrange("p (k b) -> p k b", k=4),
                                        ALU.add, ALU.mult))
            y.wait(v, 0)
            y.up(v.tensor_scalar(cT[:, :, :], cT[:, :, :], 0.5, None, ALU.mult))
            s_p["pe"].wait(v, 2)
            v.tensor_tensor(rb[:, 0, :], rb[:, 0, :], psY[:, 0:256], ALU.add)
            v.tensor_tensor(rb[:, 2, :], rb[:, 2, :], psY[:, 256:512], ALU.add)
            v.tensor_tensor(rb[:, 3, :], rb[:, 3, :], psT[1][:, 0:256], ALU.add)
            for l in range(2):
                for n in range(3):
                    for k in range(2):
                        ins = v.tensor_scalar(W[l][n][:, k, :], W[l][n][:, k, :], col[:, l, k:k + 1], None, ALU.mult)
            z.up(ins)
            z.wait(v, 7)
            s_p["pe"].wait(v, 3)
            f = 2
            for l in range(2):
                for d in range(2):
                    e_ = psT[0][:, 0:8 * B].rearrange("p (l o b) -> p l o b", l=2, o=4)
                    y.up(v.tensor_scalar(sc, e_[:, l, d, :], col[:, l, 8 + d:9 + d], 1.0, ALU.add, ALU.add))
                    y.wait(v, f)
                    y.up(v.tensor_scalar(FA[:, l, d, :], sc, col[:, l, 12 + d:13 + d], 0.5, ALU.mult, ALU.mult))
                    y.up(v.scalar_tensor_tensor(FB[:, l, d, :], sc, col[:, l, 14 + d:15 + d], e_[:, l, 2 + d, :],
                                                ALU.mult, ALU.add))
                    y.wait(v, f + 2)
                    y.up(v.tensor_scalar(FB[:, l, d, :], FB[:, l, d, :], col[:, l, 10 + d:11 + d], 0.5,
                                         ALU.add, ALU.mult))
                    f += 4
            for k in range(4):
                y.up(v.tensor_copy(BD[:, k, 128:136], diag[:, 0:128].rearrange("p (h e) -> p h e", e=DH)[:, :, 0]))
            y.wait(v, f + 3)

            def csplit(n, hf):
                s_ct.wait(v, n, hf + 1)
                s_cin[hf].wait(v, n - 1)
                b4 = 4 * hf
                s_cs.up(v.tensor_copy(cp[hf][:, 0, :], psX[0:16, 0:128]))
                s_cs.wait(v, n, b4 + 1)
                s_cs.up(v.tensor_tensor(cr[:, :], psX[0:16, 0:128], cp[hf][:, 0, :], ALU.subtract))
                s_cs.wait(v, n, b4 + 2)
                s_cs.up(v.tensor_copy(cp[hf][:, 1, :], cr[:, :]))
                s_cs.wait(v, n, b4 + 3)
                s_cs.up(v.tensor_tensor(cp[hf][:, 2, :], cr[:, :], cp[hf][:, 1, :], ALU.subtract))

            def slot(t, i):
                if i == 0 and ok(t):
                    s_x.wait(v, t)
                    s_xn.wait(v, t - 1)
                    for k in range(2):
                        s_st.up(v.bn_stats(st[:, k, :], xt[t % 2][:, k, :]))
                    for k in range(2):
                        s_st.wait(v, t, k + 1)
                        s_st.up(v.bn_aggr(mv[:, k, :], st[:, k, :]))
                if ok(t - 2):
                    n = t - 2
                    for h in (2 * i, 2 * i + 1):
                        s_sm.wait(v, n, h + 1)
                        s_ct.wait(v, n - 2)
                        s_mx.up(v.tensor_reduce(cm[n % 2][:, 2 * h:2 * h + 2],
                                                psM[h % 2][:, :].rearrange("p (k t) -> p k t", k=2),
                                                AX.X, ALU.max, negate=True))
                if i == 0 and ok(t - 3):
                    csplit(t - 3, 1)
                if i in (1, 2) and ok(t - 4):
                    n, k = t - 4, i - 1
                    s_yt.wait(v, n, k + 1)
                    s_y.wait(v, n - 1, k + 1)
                    ps = psX[:, :].rearrange("p (h d) -> p h d", d=32)
                    s_yd.up(v.reciprocal(rd[:, :], ps[:, :, 16]))
                    s_yd.wait(v, n, 4 * k + 1)
                    s_yd.up(v.tensor_tensor(yr[:, k, :].rearrange("p (h d) -> p h d", d=DH), ps[:, :, 0:16],
                                            rd[:, :].rearrange("p (h a) -> p h a", a=1).to_broadcast([128, H, DH]),
                                            ALU.mult))
                    s_yd.wait(v, n, 4 * k + 2)
                    s_yd.up(v.bn_stats(st[:, 2 + k, :], yr[:, k, :]))
                    s_yd.wait(v, n, 4 * k + 3)
                    s_yd.up(v.bn_aggr(mv[:, 2 + k, :], st[:, 2 + k, :]))
                if i in (4, 6) and ok(t):
                    w = (i - 4) // 2
                    s_qf.wait(v, t, w + 1)
                    s_qo[w].wait(v, t - 1)
                    s_hi.up(v.tensor_copy(qp[w][:, 0, :, :], qf[w][:, :, :]))
                if i == 5 and ok(t - 2):
                    csplit(t - 2, 0)
                if i in (5, 7) and ok(t):
                    w = (i - 5) // 2
                    s_rf.wait(v, t, w + 1)
                    s_mi.up(v.tensor_copy(qp[w][:, 1, :, :], rf[:, :, :]))
                if i == 7 and ok(t):
                    s_vm.wait(v, t)
                    s_v.wait(v, t - 1)
                    s_vt.up(v.tensor_tensor(vt[:, :, :], psX[:, :].rearrange("p (k d) -> p k d", k=2), vb0,
                                            ALU.add))
            each(slot)
            phase2_dve(v)

        @block.tensor
        def _(pe):
            pe.wait_ge(s_ld, pre["ld"])
            done = s_p["pe"]
            s_p["mneg"].wait(pe, 1)
            for n, src in enumerate((mrow, keep)):
                for k in range(2):
                    c = 2 * B * n + B * k
                    ins = pe.transpose(psX[:, c:c + B], src[:, 128 * k:128 * k + 128], ident[0:B, 0:B])
            done.up(ins)
            for k in range(4):
                ins = pe.transpose(psM[1][:, B * k:B * k + B], cond_sb[:, 128 * k:128 * k + 128], ident[0:B, 0:B])
            done.up(ins)
            for n, (l, w) in enumerate(((0, 0), (0, 1), (1, 1))):
                for o in range(2):
                    for k in range(2):
                        pe.matmul(psM[0][:, 2 * n + o:2 * n + o + 1], W[l][w][:, k, 128 * o:128 * o + 128],
                                  col[:, l, 2 + k:3 + k], start=(k == 0), stop=(k == 1))
            for dst, l, w in ((psY[:, 0:256], 0, 2), (psY[:, 256:512], 1, 0), (psT[1][:, 0:256], 1, 2)):
                for k in range(2):
                    ins = pe.matmul(dst, col[:, l, 2 + k:3 + k].to_broadcast([128, 128]), W[l][w][:, k, :],
                                    start=(k == 0), stop=(k == 1))
            done.up(ins)
            s_p["film"].wait(pe, 1)
            for l in range(2):
                for o in range(4):
                    c = B * (4 * l + o)
                    for k in range(4):
                        ins = pe.matmul(psT[0][:, c:c + B], EW[:, l, k, 128 * o:128 * o + 128], cT[:, k, :],
                                        start=(k == 0), stop=(k == 3))
            done.up(ins)
            s_p["ve0"].wait(pe, 7)
            s_p["act"].wait(pe, 2)
            s_p["pool"].wait(pe, 1)
            s_p["film"].wait(pe, 21)

            read = []

            def take(*by):
                if read:
                    read[0].wait(pe, *read[1:])
                read[:] = by

            def ctr(n, hf):
                s_mx.wait(pe, n, 8 * hf + 8)
                s_ct.up(pe.transpose(psX[0:16, 0:128], cm[n % 2][:, 16 * hf:16 * hf + 16], ident[:, :]))

            def slot(t, i):
                n = t - 3
                if ok(n):
                    G = 8 * n + i
                    if i == 0:
                        s_in.wait(pe, n)
                        s_cin[0].wait(pe, n)
                    if i == 4:
                        s_cin[1].wait(pe, n)
                    if G >= 2:
                        pe.wait_ge(s_ex.sem, G - 1)
                    for hh in range(2):
                        h = 2 * i + hh
                        for m in range(2):
                            ins = pe.matmul(psT[G % 2][:, 512 * hh + 256 * m:512 * hh + 256 * m + 256],
                                            Ks[n % 3][0:KS, h, 128 * m:128 * m + 128], Qs[n % 3][0:KS, h, :],
                                            start=True, stop=True)
                    s_sT.up(ins)
                if i % 2 == 0:
                    n, gr = (t - 3, i // 2 - 1) if i else (t - 4, 3)
                    if ok(n):
                        s_ex.wait(pe, n, 2 * gr + 2)
                        s_v.wait(pe, n)
                        if 4 * n + gr:
                            pe.wait_ge(s_ye.sem, 4 * n + gr)
                        for m in range(2):
                            for j in range(4):
                                Pj = P[(8 * n + 2 * gr + j // 2) % 4]
                                c0 = 512 * (j % 2) + 256 * m
                                ins = pe.matmul(psY[32 * j:32 * j + 32, 0:T], Vp[n % 4][:, m, 4 * gr + j, :],
                                                Pj[:, c0:c0 + 256], start=(m == 0), stop=(m == 1))
                        s_pv.up(ins)
                n = t - 2
                if ok(n):
                    if i == 0:
                        s_in.wait(pe, n)
                    for h in (2 * i, 2 * i + 1):
                        if H * n + h >= 2:
                            pe.wait_ge(s_mx.sem, H * n + h - 1)
                        for k in range(2):
                            ins = pe.matmul(psM[h % 2][:, 256 * k:256 * k + 256],
                                            Qs[n % 3][0:KM, h, 128 * k:128 * k + 128], Ks[n % 3][0:KM, h, :],
                                            start=True, stop=True)
                        s_sm.up(ins)
                if i == 0 and ok(t - 3):
                    take(s_cs, t - 3, 6)
                    ctr(t - 3, 1)
                if i in (1, 2) and ok(t - 4):
                    n, k = t - 4, i - 1
                    s_ye.wait(pe, n)
                    take(s_yd, n, 4 * k + 2)
                    for q in range(4):
                        ins = pe.transpose(psX[:, 128 * q:128 * q + 128], yT[:, q, 128 * k:128 * k + 128], ident[:, :])
                    s_yt.up(ins)
                if i == 3 and ok(t):
                    s_xn.wait(pe, t)
                    take(s_xT, t, 1)
                    for d in range(2):
                        for k in range(2):
                            ins = pe.transpose(psX[:, 256 * d + 128 * k:256 * d + 128 * k + 128],
                                               xn[:, k, 128 * d:128 * d + 128], ident[:, :])
                    s_xtr.up(ins)
                if i in (4, 6) and ok(t):
                    w = (i - 4) // 2
                    s_xT.wait(pe, t)
                    take(s_qf, t, w + 1)
                    for o in range(2):
                        for k in range(2):
                            ins = pe.matmul(psX[:, 256 * o:256 * o + 256], W[0][w][:, k, 128 * o:128 * o + 128],
                                            xT[:, k, :], start=(k == 0), stop=(k == 1))
                    s_qm.up(ins)
                if i == 5 and ok(t - 2):
                    take(s_cs, t - 2, 2)
                    ctr(t - 2, 0)
                if i == 7 and ok(t):
                    take(s_vt, t, 1)
                    for k in range(2):
                        for d in range(2):
                            ins = pe.matmul(psX[:, 256 * k:256 * k + 256], xT[:, d, 128 * k:128 * k + 128],
                                            W[0][2][:, d, :], start=(d == 0), stop=(d == 1))
                    s_vm.up(ins)
            each(slot)
            phase2_pe(pe)


def layer(inputs, l, names):
    return [inputs[f"L{l}_cond_{n}"] for n in names.split()]


def packed(inputs):
    w = [layer(inputs, 0, "q_w k_w v_w out_w"), layer(inputs, 1, "Wq Wk Wv film_out_W")]
    w = np.stack([np.stack([np.asarray(a).reshape(2, 128, D) for a in ws]) for ws in w])
    e = np.stack([np.asarray(layer(inputs, 0, "emb_w")[0]), np.asarray(layer(inputs, 1, "film_emb_W")[0])])
    c = [layer(inputs, 0, "norm_w norm_b q_b k_b emb_b sb_norm_w sb_norm_b"),
         layer(inputs, 1, "norm_scale norm_bias bq bk film_emb_b film_norm_scale film_norm_bias")]
    c = np.stack([np.concatenate([np.asarray(a).reshape(-1, 128) for a in cs]) for cs in c])
    r = np.stack([np.asarray(a) for a in layer(inputs, 0, "v_b out_b") + layer(inputs, 1, "bq bv film_out_b")])
    return {
        "weights": np.ascontiguousarray(w.transpose(3, 0, 1, 2, 4)),
        "emb": np.ascontiguousarray(e.reshape(2, 4, 128, 2 * D).transpose(2, 0, 1, 3)),
        "cols": np.ascontiguousarray(c.transpose(2, 0, 1)),
        "rows": r,
        "ident": np.eye(128, dtype=np.float32),
        "diag": np.kron(np.eye(128 // DH, dtype=np.float32), np.ones((DH, DH), np.float32)),
    }


def kernel(**inputs):
    import concourse.bacc as bacc
    from concourse.bass_utils import run_bass_kernel_spmd

    nc = bacc.Bacc("TRN2", target_bir_lowering=False, num_devices=1)
    given = {
        "x": inputs["x"], "cond": inputs["cond_2048"], "mask_f": inputs["mask_BxS_ff1"],
        "mask_i": inputs["mask_BxS_ik0"],
    }
    arrays, args = {}, []
    for name, a in (given | packed(inputs)).items():
        a = np.ascontiguousarray(a)
        arrays[f"in_{name}"] = a
        args.append(nc.dram_tensor(f"in_{name}", a.shape, mybir.dt.from_np(a.dtype), kind="ExternalInput").ap())
    args.append(nc.dram_tensor("out_0", (B, T, D), F32, kind="ExternalOutput").ap())
    bass_cond_seq_kernel(nc, *args)
    r = run_bass_kernel_spmd(nc, [arrays], core_ids=[0])
    return r.results[0]["out_0"]
```

```python
from contextlib import ExitStack

import numpy as np

import concourse.bass as bass
from concourse import mybir

F32 = mybir.dt.float32
BF16 = mybir.dt.bfloat16
I32 = mybir.dt.int32
ALU = mybir.AluOpType
ACT = mybir.ActivationFunctionType
AX = mybir.AxisListType

B = 32
T = 256
D = 256
H = 16
DH = 16
E = 512
EPS = 1e-5
NEG = -1.0e30
ONES = 0x3F803F80
KM = 99
KS = 102


class Count:

    def __init__(self, sem, per=1):
        self.sem, self.per = sem, per

    def up(self, ins):
        ins.then_inc(self.sem, 1)

    def wait(self, eng, n, k=None):
        if n >= 0:
            eng.wait_ge(self.sem, self.per * n + (self.per if k is None else k))


class Landed:

    def __init__(self, sems, per=1):
        self.sems, self.per = sems, per

    def up(self, ins, n):
        ins.then_inc(self.sems[n % len(self.sems)], 16)

    def wait(self, eng, n):
        if n >= 0:
            eng.wait_ge(self.sems[n % len(self.sems)], 16 * self.per * (n // len(self.sems) + 1))


def bass_cond_seq_kernel(nc, x, cond, mask_f, mask_i, weights, emb, cols, rows, ident_d, diag_d, out):
    qd = nc.dram_tensor("q_parts", (B, 3 * DH, H * T), BF16, kind="Internal").ap()
    kd = nc.dram_tensor("k_parts", (B, 3 * DH, H * T), BF16, kind="Internal").ap()
    md = nc.dram_tensor("mask_parts", (B, 3, T), BF16, kind="Internal").ap()

    nd = nc.dram_tensor("key_mask", (B, T), F32, kind="Internal").ap()

    with ExitStack() as ctx:
        def sb(name, shape, dt=F32):
            return ctx.enter_context(nc.sbuf_tensor("sb_" + name, shape, dt))

        def sem(name):
            return ctx.enter_context(nc.semaphore(name))

        def count(name, per=1):
            return Count(sem(name), per)

        def landed(name, ring, per=1):
            return Landed([sem(f"{name}{i}") for i in range(ring)], per)

        psT = [ctx.enter_context(nc.psum_tensor(f"psT{i}", [128, 1024], F32)) for i in range(2)]
        psM = [ctx.enter_context(nc.psum_tensor(f"psM{i}", [128, 512], F32)) for i in range(2)]
        psY = ctx.enter_context(nc.psum_tensor("psY", [128, 512], F32))
        psX = ctx.enter_context(nc.psum_tensor("psX", [128, 512], F32))

        Y = sb("Y", [128, max(2 * B, 28), D])
        Wt = [sb(f"W{l}", [128, 4, 2, D]) for l in range(2)]
        W = [[Wt[l][:, n, :, :] for n in range(4)] for l in range(2)]
        EW = Y[:, 0:16, :].rearrange("p (l k a) n -> p l k (a n)", l=2, k=4)
        Qs = [sb(f"Qs{i}", [128, H, T], BF16) for i in range(3)]
        Ks = [sb(f"Ks{i}", [128, H, T], BF16) for i in range(3)]
        P = [sb(f"P{i}", [128, 1024]) for i in range(4)]
        Vp = [sb(f"Vp{i}", [128, 2, H, 32]) for i in range(4)]
        ident = sb("ident", [128, 128])
        xt = [sb(f"xt{i}", [128, 2, D]) for i in range(2)]
        xn = sb("xn", [128, 2, D])
        xT = sb("xT", [128, 2, T])
        qf = [sb(f"qf{i}", [128, 2, T]) for i in range(2)]
        rf = sb("rf", [128, 2, T])
        qp = [sb(f"qp{i}", [128, 3, 2, T], BF16) for i in range(2)]
        vt = sb("vt", [128, 2, D])
        yT = sb("yT", [128, 4, T])
        yr = sb("yr", [128, 2, D])
        rb = sb("rb", [128, 5, D])
        vb0, ob0, qb1, vb1, ob1 = (rb[:, r:r + 1, :].to_broadcast([128, 2, D]) for r in range(5))
        cm = [sb(f"cm{i}", [128, 2 * H]) for i in range(2)]
        cp = [sb(f"cp{i}", [16, 3, 128], BF16) for i in range(2)]
        cr = sb("cr", [16, 128])
        st = sb("st", [128, 4, 6])
        mv = sb("mv", [128, 4, 2])
        ve = sb("ve", [128, 4])
        rs = sb("rs", [128, 4])
        nm = sb("nm", [128, 4])
        rd = sb("rd", [128, H])
        rd2 = sb("rd2", [128, 2, 2, 8])
        xT2 = sb("xT2", [128, 2, T])
        xT1 = [xT[:, :, :], xT2[:, :, :]]
        ph = sb("ph", [128, 2])
        bq = sb("bq", [128, 6])
        col = sb("col", [128, 2, 16])
        cT = sb("cT", [128, 4, B])
        cond_sb = Y[0:B, 16:18, :].rearrange("b a n -> b (a n)")
        tc = Y[:, 18, 0:4 * B].rearrange("p (k b) -> p k b", k=4)
        sc = Y[:, 19, 0:B]
        FA = sb("FA", [128, 2, 2, B])
        FB = sb("FB", [128, 2, 2, B])
        kT = sb("kT", [128, 2, B])
        mrow, mr2, mr3, keep = (Y[0:B, n, :] for n in range(20, 24))
        irow = Y[0:B, 24, :].bitcast(I32)
        mp = Y[0:B, 26:28, :].rearrange("b a n -> b (a n)").bitcast(BF16)[:, 0:3 * T].rearrange("b (c t) -> b c t", c=3)
        mT = sb("mT", [128, 2, B])
        diag = sb("diag", [128, 128])
        BD = sb("BD", [128, 4, 136])
        qm = sb("qm", [128, 2 * H])
        kx = sb("kx", [128, 2])
        ksum = sb("ksum", [128, 2])
        kd2 = sb("kd2", [128, 2])

        s_ld = sem("s_ld")
        n_ld = [0]
        s_set = sem("s_set")
        s_x = landed("s_x", 2)
        s_st = count("s_st", 4)
        s_rs = count("s_rs", 4)
        s_xn = count("s_xn")
        s_xtr = count("s_xtr")
        s_xT = count("s_xT")
        s_qm = count("s_qm", 2)
        s_qf = count("s_qf", 2)
        s_hi = count("s_hi", 2)
        s_rf = count("s_rf", 2)
        s_mi = count("s_mi", 2)
        s_lo = count("s_lo", 2)
        s_qo = [landed("s_qo", 2), landed("s_ko", 2)]
        s_in = landed("s_in", 3, 7)
        s_vm = count("s_vm")
        s_vt = count("s_vt")
        s_v = count("s_v")
        s_sm = count("s_sm", H)
        s_mx = count("s_mx", H)
        s_ct = count("s_ct", 2)
        s_cs = count("s_cs", 8)
        s_cin = [landed("s_ca", 2, 3), landed("s_cb", 2, 3)]
        s_sT = count("s_sT", 8)
        s_ex = count("s_ex", 8)
        s_pv = count("s_pv", 4)
        s_ye = count("s_ye", 4)
        s_yt = count("s_yt", 2)
        s_yd = count("s_yd", 8)
        s_yr = count("s_yr", 8)
        s_y = count("s_y", 2)

        block = ctx.enter_context(nc.Block())
        pre = {}

        def each(fn):
            for t in range(B + 4):
                for i in range(8):
                    fn(t, i)

        def ok(n):
            return 0 <= n < B

        s_p = {k: count("p_" + k) for k in ("ve0", "pe", "act", "pool", "mneg", "film")}
        s_md = landed("s_md", 1, 2)

        PE = ((0, "f0"), (1, "o0"), (2, "k"), (3, "y"), (4, "f1"), (5, "o1"), (1, "tr"), (2, "v"), (2, "kt"),
              (1, "q"), (2, "qt"), (2, "kv"))
        AC = ((4, "yn"), (0, "u0"), (0, "t0"), (1, "xn"), (2, "ke"), (1, "xT"), (4, "u1"), (2, "kn"), (2, "vk"),
              (4, "t1"), (2, "qe"))
        DV = ((2, "dq"), (3, "bd"), (5, "h1"), (1, "x1"), (1, "st0"), (2, "dk"), (2, "mk"), (0, "h0"), (2, "mq"),
              (2, "ken"), (5, "ob"), (2, "dv"), (3, "yd"), (3, "st1"))
        GP = ((0, "xb"), (4, "rs1"), (2, "xo"), (1, "rs0"), (2, "qs"))
        ROUNDS = B + 5
        room = [r[:, :, :].rearrange("p h t -> p (h t)").bitcast(F32)[:, 512 * u:512 * u + 512]
                for r in Qs + Ks for u in range(4)]
        room += [r[:, 512 * u:512 * u + 512] for r in P for u in range(2)]
        room += [r[:, u, :, :].rearrange("p h d -> p (h d)") for r in Vp for u in range(2)]

        def unit():
            return room.pop(0).rearrange("p (k t) -> p k t", k=2)

        xr = [unit() for _ in range(3)]
        x1 = [unit() for _ in range(6)]
        kr = [unit() for _ in range(2)]
        ub, th, hb = ([[unit() for _ in range(2)] for _ in range(2)] for _ in range(3))
        xb, km, ke, ken, v1, ob = (unit() for _ in range(6))
        tq, kn, vk, qe, yn = ([unit() for _ in range(2)] for _ in range(5))
        R = [psT[0][:, 0:512], psT[0][:, 512:1024], psT[1][:, 0:512], psT[1][:, 512:1024],
             psM[0][:, :], psM[1][:, :], psY[:, :], psX[:, :]]
        BANK = {"f0": 7, "f1": 3, "o0": 6, "o1": 2, "k": 4, "tr": 5, "v": 4, "kt": 5, "q": 3, "qt": 5, "kv": 4}

        def tiles(step):
            return R[BANK[step]].rearrange("p (k t) -> p k t", k=2)

        e = {name: count("e_" + name, {"st0": 4, "st1": 4, "rs0": 4, "rs1": 4, "yd": 2, "ken": 2}.get(name, 1))
             for order in (PE, AC, DV, GP) for _, name in order}
        e_xr = landed("e_xr", 3)
        e_kr = landed("e_kr", 2)
        e_out = landed("e_out", 1)

        def rounds(steps, order):
            for t in range(ROUNDS):
                for lag, name in order:
                    if 0 <= t - lag < B:
                        steps[name](t - lag)

        def phase2_sp(sp):
            s_y.wait(sp, B - 1)

            def load(n):
                if n < B:
                    e["xb"].wait(sp, n - 3)
                    e_xr.up(sp.dma_start(xr[n % 3], x[n].rearrange("(k p) d -> p k d", p=128)), n)
            load(0)
            load(1)
            for t in range(ROUNDS):
                load(t + 2)
                if t >= 1 and t - 1 < B:
                    n = t - 1
                    e["dk"].wait(sp, n - 2)
                    e_kr.up(sp.dma_start(kr[n % 2][:, 0, :], nd[n:n + 1, :].to_broadcast([128, T])), n)
                if t >= 5:
                    n = t - 5
                    e["ob"].wait(sp, n)
                    e_out.up(sp.dma_start(out[n].rearrange("(k p) d -> p k d", p=128), ob), n)
            e_out.wait(sp, B - 1)

        def phase2_gpsimd(g):
            s_y.wait(g, B - 1)

            def xb_(n):
                e_xr.wait(g, n)
                e["x1"].wait(g, n - 1)
                e["xb"].up(g.tensor_tensor(xb, xr[n % 3], ob0, ALU.add))

            def xo_(n):
                e["xn"].wait(g, n)
                e["xo"].up(g.tensor_tensor(x1[n % 6], x1[n % 6], ob1, ALU.add))

            def rs_(l, used):
                def f(n):
                    k, sig = slice(2 * l, 2 * l + 2), e[f"rs{l}"]
                    e[f"st{l}"].wait(g, n)
                    e[used].wait(g, n - 1)
                    sig.up(g.tensor_scalar(ve[:, k], mv[:, k, 1], EPS, None, ALU.add))
                    sig.wait(g, n, 1)
                    sig.up(g.tensor_tensor(rs[:, k], ve[:, k], ph[:, :], ALU.pow))
                    sig.wait(g, n, 2)
                    sig.up(g.tensor_tensor(ve[:, k], mv[:, k, 0], rs[:, k], ALU.mult))
                    sig.wait(g, n, 3)
                    sig.up(g.tensor_scalar(nm[:, k], ve[:, k], -1.0, None, ALU.mult))
                return f

            def qs_(n):
                e["mq"].wait(g, n)
                q4 = tq[n % 2].rearrange("p k (h d) -> p (k h) d", d=DH)
                e["qs"].up(g.tensor_tensor(
                    q4, q4, qm[:, :].rearrange("p (h a) -> p h a", a=1).to_broadcast([128, 2 * H, DH]), ALU.add))
            rounds({"xb": xb_, "xo": xo_, "rs0": rs_(0, "xn"), "rs1": rs_(1, "yn"), "qs": qs_}, GP)

        def phase2_act(a):
            s_y.wait(a, B - 1)

            def u_(l):
                def f(n):
                    e[f"f{l}"].wait(a, n)
                    e[f"h{l}"].wait(a, n - 2)
                    for d in range(2):
                        ins = a.activation(ub[l][n % 2][:, d, :], tiles(f"f{l}")[:, d, :], ACT.Identity,
                                           bias=FB[:, l, d, n:n + 1], scale=FA[:, l, d, n:n + 1])
                    e[f"u{l}"].up(ins)
                return f

            def t_(l):
                def f(n):
                    e[f"u{l}"].wait(a, n)
                    e[f"h{l}"].wait(a, n - 2)
                    e[f"t{l}"].up(a.activation(th[l][n % 2], ub[l][n % 2], ACT.Tanh))
                return f

            def xn_(n):
                e["rs0"].wait(a, n)
                e["tr"].wait(a, n - 1)
                for i in range(2):
                    ins = a.activation(xn[:, i, :], x1[n % 6][:, i, :], ACT.Identity, bias=nm[:, i:i + 1],
                                       scale=rs[:, i:i + 1])
                e["xn"].up(ins)

            def yn_(n):
                e["rs1"].wait(a, n)
                e["f1"].wait(a, n - 2)
                for i in range(2):
                    ins = a.activation(yn[n % 2][:, i, :], yr[:, i, :], ACT.Identity, bias=nm[:, 2 + i:3 + i],
                                       scale=rs[:, 2 + i:3 + i])
                e["yn"].up(ins)

            def xT_(n):
                e["tr"].wait(a, n)
                for s in "qkv":
                    e[s].wait(a, n - 2)
                e["xT"].up(a.activation(xT1[n % 2], tiles("tr"), ACT.Identity))

            def ke_(n):
                e["mk"].wait(a, n)
                e["ken"].wait(a, n - 1)
                for i in range(2):
                    ins = a.activation(ke[:, i, :], km[:, i, :], ACT.Exp, bias=kx[:, i:i + 1],
                                       accum_out=ksum[:, i:i + 1])
                e["ke"].up(ins)

            def vk_(n):
                e["dv"].wait(a, n)
                e["kv"].wait(a, n - 2)
                for i in range(2):
                    ins = a.activation(vk[n % 2][:, i, :], v1[:, i, :], ACT.Identity, scale=kT[:, i, n:n + 1])
                e["vk"].up(ins)

            def qe_(n):
                e["qt"].wait(a, n)
                e["y"].wait(a, n - 2)
                e["qe"].up(a.activation(qe[n % 2], tiles("qt"), ACT.Exp))

            def kn_(n):
                e["kt"].wait(a, n)
                e["kv"].wait(a, n - 2)
                e["kn"].up(a.activation(kn[n % 2], tiles("kt"), ACT.Identity))
            rounds({"u0": u_(0), "u1": u_(1), "t0": t_(0), "t1": t_(1), "xn": xn_, "yn": yn_, "xT": xT_, "ke": ke_,
                    "vk": vk_, "qe": qe_, "kn": kn_}, AC)

        def phase2_dve(v):
            s_y.wait(v, B - 1)

            def h_(l):
                def f(n):
                    e[f"t{l}"].wait(v, n)
                    e[f"o{l}"].wait(v, n - 2)
                    e[f"h{l}"].up(v.scalar_tensor_tensor(hb[l][n % 2], th[l][n % 2], 1.0, ub[l][n % 2],
                                                         ALU.add, ALU.mult))
                return f

            def x1_(n):
                e["o0"].wait(v, n)
                e["xb"].wait(v, n)
                e["ob"].wait(v, n - 6)
                e["x1"].up(v.tensor_tensor(x1[n % 6], tiles("o0"), xb, ALU.add))

            def st_(l, src, after, used):
                def f(n):
                    e[after].wait(v, n)
                    e[used].wait(v, n - 1)
                    for i in range(2):
                        e[f"st{l}"].up(v.bn_stats(st[:, 2 * l + i, :], src(n)[:, i, :]))
                    for i in range(2):
                        e[f"st{l}"].wait(v, n, 1 + i)
                        e[f"st{l}"].up(v.bn_aggr(mv[:, 2 * l + i, :], st[:, 2 * l + i, :]))
                return f

            def dq_(n):
                e["q"].wait(v, n)
                e["qt"].wait(v, n - 2)
                e["dq"].up(v.tensor_tensor(tq[n % 2], tiles("q"), qb1, ALU.add))

            def mq_(n):
                e["dq"].wait(v, n)
                e["qs"].wait(v, n - 1)
                e["mq"].up(v.tensor_reduce(qm[:, :], tq[n % 2].rearrange("p k (h d) -> p (k h) d", d=DH), AX.X,
                                           ALU.max, negate=True))

            def dk_(n):
                e["k"].wait(v, n)
                e_kr.wait(v, n)
                e["ke"].wait(v, n - 1)
                for i in range(2):
                    ins = v.scalar_tensor_tensor(km[:, i, :], tiles("k")[:, i, :], bq[:, 4 + i:5 + i],
                                                 kr[n % 2][:, 0, :], ALU.add, ALU.add)
                e["dk"].up(ins)

            def mk_(n):
                e["dk"].wait(v, n)
                e["ke"].wait(v, n - 1)
                e["mk"].up(v.tensor_reduce(kx[:, :], km, AX.X, ALU.max, negate=True))

            def ken_(n):
                e["ke"].wait(v, n)
                e["kt"].wait(v, n - 1)
                e["ken"].up(v.reciprocal(kd2[:, :], ksum[:, :]))
                e["ken"].wait(v, n, 1)
                for i in range(2):
                    ins = v.tensor_scalar(ken[:, i, :], ke[:, i, :], kd2[:, i:i + 1], None, ALU.mult)
                e["ken"].up(ins)

            def dv_(n):
                e["v"].wait(v, n)
                e["vk"].wait(v, n - 1)
                e["dv"].up(v.tensor_tensor(v1, tiles("v"), vb1, ALU.add))

            def bd_(n):
                e["kv"].wait(v, n)
                e["y"].wait(v, n - 2)
                e["bd"].up(v.tensor_tensor(BD[:, 2 * (n % 2):2 * (n % 2) + 2, 0:128], tiles("kv")[:, :, 0:128],
                                           diag[:, :].rearrange("p (a e) -> p a e", a=1).to_broadcast([128, 2, 128]),
                                           ALU.mult))

            def yd_(n):
                e["y"].wait(v, n)
                e["yn"].wait(v, n - 1)
                ps = psT[0][:, :].rearrange("p (i c) -> p i c", i=2)[:, :, 0:272]\
                    .rearrange("p i (f c) -> p i f c", f=2)
                for i in range(2):
                    ins = v.reciprocal(rd2[:, i, :, :], ps[:, i, :, 128:136])
                e["yd"].up(ins)
                e["yd"].wait(v, n, 1)
                for i in range(2):
                    for f in range(2):
                        ins = v.tensor_tensor(
                            yr[:, i, 128 * f:128 * f + 128].rearrange("p (h e) -> p h e", e=DH),
                            ps[:, i, f, 0:128].rearrange("p (h e) -> p h e", e=DH),
                            rd2[:, i, f, :].rearrange("p (h a) -> p h a", a=1).to_broadcast([128, 8, DH]), ALU.mult)
                e["yd"].up(ins)

            def ob_(n):
                e["o1"].wait(v, n)
                e["xo"].wait(v, n)
                e_out.wait(v, n - 1)
                e["ob"].up(v.tensor_tensor(ob, tiles("o1"), x1[n % 6], ALU.add))
            rounds({"h0": h_(0), "h1": h_(1), "x1": x1_, "st0": st_(0, lambda n: x1[n % 6], "x1", "rs0"),
                    "st1": st_(1, lambda n: yr, "yd", "rs1"), "dq": dq_, "mq": mq_, "dk": dk_, "mk": mk_,
                    "ken": ken_, "dv": dv_, "bd": bd_, "yd": yd_, "ob": ob_}, DV)

        def phase2_pe(pe):
            s_y.wait(pe, B - 1)
            read = {}

            def take(bank, step, n, k=None):
                if bank in read:
                    m = read[bank]
                    e[m[0]].wait(pe, *m[1:])
                read[bank] = (step, n, k)

            def turned(step, n, reader, src):
                take(BANK[step], reader, n)
                for a in range(2):
                    for b in range(2):
                        ins = pe.transpose(tiles(step)[:, a, 128 * b:128 * b + 128],
                                           src[b][:, 128 * a:128 * a + 128], ident[:, :])
                e[step].up(ins)

            def natural(step, n, reader, lhs, w):
                take(BANK[step], reader, n)
                for i in range(2):
                    for d in range(2):
                        ins = pe.matmul(tiles(step)[:, i, :], lhs[:, d, 128 * i:128 * i + 128], w[:, d, :],
                                        start=(d == 0), stop=(d == 1))
                e[step].up(ins)

            def f0_(n):
                turned("f0", n, "u0", [Y[:, 2 * n + i, :] for i in range(2)])

            def f1_(n):
                e["yn"].wait(pe, n)
                turned("f1", n, "u1", [yn[n % 2][:, i, :] for i in range(2)])

            def tr_(n):
                e["xn"].wait(pe, n)
                turned("tr", n, "xT", [xn[:, i, :] for i in range(2)])

            def qt_(n):
                e["qs"].wait(pe, n)
                turned("qt", n, "qe", [tq[n % 2][:, i, :] for i in range(2)])

            def kt_(n):
                e["ken"].wait(pe, n)
                turned("kt", n, "kn", [ken[:, i, :] for i in range(2)])

            def o_(l):
                def f(n):
                    e[f"h{l}"].wait(pe, n)
                    natural(f"o{l}", n, ("x1", "ob")[l], hb[l][n % 2], W[l][3])
                return f

            def q_(n):
                e["xT"].wait(pe, n)
                natural("q", n, "dq", xT1[n % 2], W[1][0])

            def v_(n):
                e["xT"].wait(pe, n)
                natural("v", n, "dv", xT1[n % 2], W[1][2])

            def k_(n):
                e["xT"].wait(pe, n)
                take(BANK["k"], "dk", n)
                for o in range(2):
                    for d in range(2):
                        ins = pe.matmul(tiles("k")[:, o, :], W[1][1][:, d, 128 * o:128 * o + 128],
                                        xT1[n % 2][:, d, :], start=(d == 0), stop=(d == 1))
                e["k"].up(ins)

            def kv_(n):
                e["kn"].wait(pe, n)
                e["vk"].wait(pe, n)
                take(BANK["kv"], "bd", n)
                for f in range(2):
                    for i in range(2):
                        ins = pe.matmul(tiles("kv")[:, f, 0:128], vk[n % 2][:, i, 128 * f:128 * f + 128],
                                        kn[n % 2][:, i, 128 * f:128 * f + 128], start=(i == 0), stop=(i == 1))
                e["kv"].up(ins)

            def y_(n):
                e["bd"].wait(pe, n)
                e["qe"].wait(pe, n)
                for i in range(2):
                    take(i, "yd", n)
                for i in range(2):
                    for f in range(2):
                        ins = pe.matmul(R[i][:, 136 * f:136 * f + 136], qe[n % 2][:, f, 128 * i:128 * i + 128],
                                        BD[:, 2 * (n % 2) + f, :], start=True, stop=True)
                e["y"].up(ins)
            rounds({"f0": f0_, "f1": f1_, "tr": tr_, "qt": qt_, "kt": kt_, "o0": o_(0), "o1": o_(1), "q": q_,
                    "v": v_, "k": k_, "kv": kv_, "y": y_}, PE)
        @block.sync
        def _(sp):
            def load(dst, src):
                sp.dma_start(dst, src).then_inc(s_ld, 16)
                n_ld[0] += 16
            load(ident[:, :], ident_d)
            load(mrow[:, :], mask_f)
            load(irow[:, :], mask_i)
            load(Wt[0][:, :, :, :], weights[:, 0])
            load(col[:, :, :], cols)
            load(rb[:, :, :], rows.rearrange("(a r) n -> a r n", a=1).to_broadcast([128, 5, D]))
            load(cond_sb, cond)
            load(EW, emb)
            load(Wt[1][:, :, :, :], weights[:, 1])
            load(diag[:, :], diag_d)
            pre["ld"] = n_ld[0]
            sp.dma_start(xt[0][:, :, :], x[0].rearrange("(k p) d -> p k d", p=128)).then_inc(s_x.sems[0], 16)
            s_p["ve0"].wait(sp, 6)
            s_p["pool"].wait(sp, 0)
            s_md.up(sp.dma_start(md.rearrange("b c t -> b (c t)"), mp[:, :, :]), 0)
            s_p["mneg"].wait(sp, 2)
            s_md.up(sp.dma_start(nd, mr3[:, :]), 0)
            s_md.wait(sp, 0)

            def c_in(n, hf):
                s_cs.wait(sp, n, 4 * hf + 4)
                for p in range(3):
                    s_cin[hf].up(sp.dma_start(
                        Qs[n % 3][KM + p:KM + p + 1, 8 * hf:8 * hf + 8, :], cp[hf][:, p, :]), n)

            def parts_out(n, w):
                s_lo.wait(sp, n, w + 1)
                s_qo[w].up(sp.dma_start((qd, kd)[w][n].rearrange("(c d) (h t) -> (d h) c t", c=3, h=8),
                                        qp[w][:, :, :, :].rearrange("p c o t -> p c (o t)")), n)

            def parts_in(n):
                s_qo[0].wait(sp, n)
                s_qo[1].wait(sp, n)
                s_sT.wait(sp, n - 3)
                for r, c, w in ((0, 0, 3), (48, 1, 2), (80, 2, 1)):
                    s_in.up(sp.dma_start(Qs[n % 3][r:r + 16 * w, :, :].rearrange("p h t -> p (h t)"),
                                         qd[n, 0:16 * w]), n)
                    s_in.up(sp.dma_start(
                        Ks[n % 3][r:r + 16 * w, :, :].rearrange("p h t -> p (h t)"),
                        kd[n, 16 * c:16 * c + 16].rearrange("(a d) t -> a d t", a=1).to_broadcast([w, DH, H * T])), n)
                s_in.up(sp.dma_start(Ks[n % 3][96:99, :, :],
                                     md[n].rearrange("c (a t) -> c a t", a=1).to_broadcast([3, H, T])), n)

            for t in range(B + 4):
                if ok(t + 1):
                    s_xn.wait(sp, t - 1)
                    s_x.up(sp.dma_start(xt[(t + 1) % 2][:, :, :], x[t + 1].rearrange("(k p) d -> p k d", p=128)), t + 1)
                if ok(t - 3):
                    c_in(t - 3, 1)
                if ok(t - 1):
                    parts_in(t - 1)
                if ok(t - 2):
                    c_in(t - 2, 0)
                if ok(t):
                    parts_out(t, 0)
                    parts_out(t, 1)
            phase2_sp(sp)

        @block.gpsimd
        def _(g):
            z = s_p["pool"]
            for i in range(3):
                ins = g.memset(Ks[i][96:KS, :, :].bitcast(I32), ONES)
            z.up(ins)
            z.wait(g, 0)
            g.memset(ph[:, :], -0.5)
            for i in range(4):
                ins = g.memset(Vp[i][:, :, :, 17:32], 0.0)
                ins = g.memset(Vp[i][:, :, :, 16:17], 1.0)
            z.up(ins)
            z.wait(g, 1)

            def rstd(c, n, k, sig, m):
                sig.up(g.tensor_scalar(ve[:, k], mv[:, k, 1], EPS, None, ALU.add))
                sig.wait(g, n, m + 1)
                sig.up(g.tensor_tensor(rs[:, k], ve[:, k], ph[:, c], ALU.pow))
                sig.wait(g, n, m + 2)
                sig.up(g.tensor_tensor(ve[:, k], mv[:, k, 0], rs[:, k], ALU.mult))
                sig.wait(g, n, m + 3)
                sig.up(g.tensor_scalar(nm[:, k], ve[:, k], -1.0, None, ALU.mult))

            def norm0(n):
                s_st.wait(g, n)
                s_xn.wait(g, n - 1)
                rstd(slice(0, 2), n, slice(0, 2), s_rs, 0)

            norm0(0)

            def slot(t, i):
                if i in (1, 2) and ok(t - 4):
                    n, k = t - 4, i - 1
                    s_yd.wait(g, n, 4 * k + 4)
                    s_y.wait(g, n - 1, k + 1)
                    rstd(slice(0, 1), n, slice(2 + k, 3 + k), s_yr, 4 * k)
                if i == 5 and ok(t + 1):
                    norm0(t + 1)
                if i in (4, 6) and ok(t):
                    w = (i - 4) // 2
                    s_qf.wait(g, t, w + 1)
                    s_qo[w].wait(g, t - 1)
                    s_hi.up(g.tensor_scalar(qp[w][:, 0, :, :], qf[w][:, :, :], 1.0, None, ALU.mult))
                    s_hi.wait(g, t, w + 1)
                    s_rf.up(g.tensor_tensor(rf[:, :, :], qf[w][:, :, :], qp[w][:, 0, :, :], ALU.subtract))
                    s_rf.wait(g, t, w + 1)
                    s_mi.up(g.tensor_scalar(qp[w][:, 1, :, :], rf[:, :, :], 1.0, None, ALU.mult))
                    s_mi.wait(g, t, w + 1)
                    s_lo.up(g.tensor_tensor(qp[w][:, 2, :, :], rf[:, :, :], qp[w][:, 1, :, :], ALU.subtract))
            each(slot)
            phase2_gpsimd(g)

        @block.scalar
        def _(a):
            done = s_p["act"]
            s_p["pe"].wait(a, 0)
            for k, dst in enumerate((mT, kT)):
                ins = a.activation(dst[:, :, :], psX[:, 2 * B * k:2 * B * k + 2 * B].rearrange("p (k b) -> p k b", k=2),
                                   ACT.Identity)
            done.up(ins)
            s_p["pe"].wait(a, 1)
            done.up(a.activation(tc, psM[1][:, 0:4 * B].rearrange("p (k b) -> p k b", k=4), ACT.Tanh, scale=0.5))
            s_p["pe"].wait(a, 2)
            for n, (l, w) in enumerate(((0, 0), (0, 1), (1, 1))):
                for o in range(2):
                    ins = a.activation(bq[:, 2 * n + o:2 * n + o + 1], psM[0][:, 2 * n + o:2 * n + o + 1], ACT.Identity,
                                       bias=col[:, l, 4 + 2 * w + o:5 + 2 * w + o])
            done.up(ins)
            done.wait(a, 2)

            def slot(t, i):
                if ok(t - 3):
                    n = t - 3
                    G = 8 * n + i
                    s_sT.wait(a, n, i + 1)
                    if G >= 4:
                        a.wait_ge(s_pv.sem, (G - 4) // 2 + 1)
                    s_ex.up(a.activation(P[G % 4][:, :], psT[G % 2][:, :], ACT.Exp))
                if i % 2 == 0:
                    n, gr = (t - 3, i // 2 - 1) if i else (t - 4, 3)
                    if ok(n):
                        s_pv.wait(a, n, gr + 1)
                        s_yt.wait(a, n - 1)
                        s_ye.up(a.activation(yT[:, gr, :], psY[:, 0:T], ACT.Identity))
                if i == 1 and ok(t):
                    s_rs.wait(a, t)
                    s_xtr.wait(a, t - 1)
                    for k in range(2):
                        ins = a.activation(xn[:, k, :], xt[t % 2][:, k, :], ACT.Identity, bias=nm[:, k:k + 1],
                                           scale=rs[:, k:k + 1])
                    s_xn.up(ins)
                if i in (3, 4) and ok(t - 4):
                    n, k = t - 4, i - 3
                    s_yr.wait(a, n, 4 * k + 4)
                    if n == 0:
                        s_p["film"].wait(a, 21)
                        s_md.wait(a, 0)
                    s_y.up(a.activation(Y[:, 2 * n + k, :], yr[:, k, :], ACT.Identity, bias=nm[:, 2 + k:3 + k],
                                        scale=rs[:, 2 + k:3 + k]))
                if i == 0 and ok(t - 1):
                    n = t - 1
                    s_vt.wait(a, n)
                    s_pv.wait(a, n - 4)
                    for k in range(2):
                        ins = a.activation(Vp[n % 4][:, k, :, 0:16],
                                           vt[:, k, :].rearrange("p (h d) -> p h d", d=DH), ACT.Identity,
                                           scale=mT[:, k, n:n + 1])
                    s_v.up(ins)
                if i == 3 and ok(t):
                    s_xtr.wait(a, t)
                    s_vm.wait(a, t - 1)
                    s_xT.up(a.activation(xT[:, :, :], psX[:, :].rearrange("p (k t) -> p k t", k=2), ACT.Identity))
                if i in (4, 6) and ok(t):
                    w = (i - 4) // 2
                    s_qm.wait(a, t, w + 1)
                    s_rf.wait(a, t - 1, w + 1)
                    for o in range(2):
                        ins = a.activation(qf[w][:, o, :], psX[:, T * o:T * o + T], ACT.Identity,
                                           bias=bq[:, 2 * w + o:2 * w + o + 1])
                    s_qf.up(ins)
            each(slot)
            phase2_act(a)

        @block.vector
        def _(v):
            z = s_p["ve0"]
            for i in range(3):
                ins = v.memset(Qs[i][96:KS, :, :].bitcast(I32), ONES)
            z.up(ins)
            v.wait_ge(s_ld, pre["ld"])
            y = s_p["mneg"]
            y.up(v.tensor_scalar(mr3[:, :], irow[:, :], 1, None, ALU.is_equal))
            y.wait(v, 0)
            y.up(v.tensor_scalar(keep[:, :], mr3[:, :], -1.0, 1.0, ALU.mult, ALU.add))
            y.wait(v, 1)
            y.up(v.tensor_scalar(mr3[:, :], mr3[:, :], NEG, None, ALU.mult))
            z.up(v.tensor_scalar(mr2[:, :], mrow[:, :], -1.0, 1.0, ALU.mult, ALU.add))
            z.wait(v, 1)
            z.up(v.tensor_scalar(mr2[:, :], mr2[:, :], -1000000.0, None, ALU.mult))
            z.wait(v, 2)
            z.up(v.tensor_copy(mp[:, 0, :], mr2[:, :]))
            z.wait(v, 3)
            z.up(v.tensor_tensor(mr2[:, :], mr2[:, :], mp[:, 0, :], ALU.subtract))
            z.wait(v, 4)
            z.up(v.tensor_copy(mp[:, 1, :], mr2[:, :]))
            z.wait(v, 5)
            z.up(v.tensor_tensor(mp[:, 2, :], mr2[:, :], mp[:, 1, :], ALU.subtract))
            y = s_p["film"]
            s_p["act"].wait(v, 1)
            y.up(v.scalar_tensor_tensor(cT[:, :, :], tc, 1.0, psM[1][:, 0:4 * B].rearrange("p (k b) -> p k b", k=4),
                                        ALU.add, ALU.mult))
            y.wait(v, 0)
            y.up(v.tensor_scalar(cT[:, :, :], cT[:, :, :], 0.5, None, ALU.mult))
            s_p["pe"].wait(v, 2)
            v.tensor_tensor(rb[:, 0, :], rb[:, 0, :], psY[:, 0:256], ALU.add)
            v.tensor_tensor(rb[:, 2, :], rb[:, 2, :], psY[:, 256:512], ALU.add)
            v.tensor_tensor(rb[:, 3, :], rb[:, 3, :], psT[1][:, 0:256], ALU.add)
            for l in range(2):
                for n in range(3):
                    for k in range(2):
                        ins = v.tensor_scalar(W[l][n][:, k, :], W[l][n][:, k, :], col[:, l, k:k + 1], None, ALU.mult)
            z.up(ins)
            z.wait(v, 7)
            s_p["pe"].wait(v, 3)
            f = 2
            for l in range(2):
                for d in range(2):
                    e_ = psT[0][:, 0:8 * B].rearrange("p (l o b) -> p l o b", l=2, o=4)
                    y.up(v.tensor_scalar(sc, e_[:, l, d, :], col[:, l, 8 + d:9 + d], 1.0, ALU.add, ALU.add))
                    y.wait(v, f)
                    y.up(v.tensor_scalar(FA[:, l, d, :], sc, col[:, l, 12 + d:13 + d], 0.5, ALU.mult, ALU.mult))
                    y.up(v.scalar_tensor_tensor(FB[:, l, d, :], sc, col[:, l, 14 + d:15 + d], e_[:, l, 2 + d, :],
                                                ALU.mult, ALU.add))
                    y.wait(v, f + 2)
                    y.up(v.tensor_scalar(FB[:, l, d, :], FB[:, l, d, :], col[:, l, 10 + d:11 + d], 0.5,
                                         ALU.add, ALU.mult))
                    f += 4
            for k in range(4):
                y.up(v.tensor_copy(BD[:, k, 128:136], diag[:, 0:128].rearrange("p (h e) -> p h e", e=DH)[:, :, 0]))
            y.wait(v, f + 3)

            def stats(n):
                s_x.wait(v, n)
                s_xn.wait(v, n - 1)
                for k in range(2):
                    s_st.up(v.bn_stats(st[:, k, :], xt[n % 2][:, k, :]))
                for k in range(2):
                    s_st.wait(v, n, k + 1)
                    s_st.up(v.bn_aggr(mv[:, k, :], st[:, k, :]))

            stats(0)

            def csplit(n, hf):
                s_ct.wait(v, n, hf + 1)
                s_cin[hf].wait(v, n - 1)
                b4 = 4 * hf
                s_cs.up(v.tensor_copy(cp[hf][:, 0, :], psX[0:16, 0:128]))
                s_cs.wait(v, n, b4 + 1)
                s_cs.up(v.tensor_tensor(cr[:, :], psX[0:16, 0:128], cp[hf][:, 0, :], ALU.subtract))
                s_cs.wait(v, n, b4 + 2)
                s_cs.up(v.tensor_copy(cp[hf][:, 1, :], cr[:, :]))
                s_cs.wait(v, n, b4 + 3)
                s_cs.up(v.tensor_tensor(cp[hf][:, 2, :], cr[:, :], cp[hf][:, 1, :], ALU.subtract))

            def slot(t, i):
                if i == 4 and ok(t + 1):
                    stats(t + 1)
                if ok(t - 2):
                    n = t - 2
                    for h in (2 * i, 2 * i + 1):
                        s_sm.wait(v, n, h + 1)
                        s_ct.wait(v, n - 2)
                        s_mx.up(v.tensor_reduce(cm[n % 2][:, 2 * h:2 * h + 2],
                                                psM[h % 2][:, :].rearrange("p (k t) -> p k t", k=2),
                                                AX.X, ALU.max, negate=True))
                if i == 0 and ok(t - 3):
                    csplit(t - 3, 1)
                if i in (1, 2) and ok(t - 4):
                    n, k = t - 4, i - 1
                    s_yt.wait(v, n, k + 1)
                    s_y.wait(v, n - 1, k + 1)
                    ps = psX[:, :].rearrange("p (h d) -> p h d", d=32)
                    s_yd.up(v.reciprocal(rd[:, :], ps[:, :, 16]))
                    s_yd.wait(v, n, 4 * k + 1)
                    s_yd.up(v.tensor_tensor(yr[:, k, :].rearrange("p (h d) -> p h d", d=DH), ps[:, :, 0:16],
                                            rd[:, :].rearrange("p (h a) -> p h a", a=1).to_broadcast([128, H, DH]),
                                            ALU.mult))
                    s_yd.wait(v, n, 4 * k + 2)
                    s_yd.up(v.bn_stats(st[:, 2 + k, :], yr[:, k, :]))
                    s_yd.wait(v, n, 4 * k + 3)
                    s_yd.up(v.bn_aggr(mv[:, 2 + k, :], st[:, 2 + k, :]))
                if i == 5 and ok(t - 2):
                    csplit(t - 2, 0)
                if i == 7 and ok(t):
                    s_vm.wait(v, t)
                    s_v.wait(v, t - 1)
                    s_vt.up(v.tensor_tensor(vt[:, :, :], psX[:, :].rearrange("p (k d) -> p k d", k=2), vb0,
                                            ALU.add))
            each(slot)
            phase2_dve(v)

        @block.tensor
        def _(pe):
            pe.wait_ge(s_ld, pre["ld"])
            done = s_p["pe"]
            s_p["mneg"].wait(pe, 1)
            for n, src in enumerate((mrow, keep)):
                for k in range(2):
                    c = 2 * B * n + B * k
                    ins = pe.transpose(psX[:, c:c + B], src[:, 128 * k:128 * k + 128], ident[0:B, 0:B])
            done.up(ins)
            for k in range(4):
                ins = pe.transpose(psM[1][:, B * k:B * k + B], cond_sb[:, 128 * k:128 * k + 128], ident[0:B, 0:B])
            done.up(ins)
            for n, (l, w) in enumerate(((0, 0), (0, 1), (1, 1))):
                for o in range(2):
                    for k in range(2):
                        pe.matmul(psM[0][:, 2 * n + o:2 * n + o + 1], W[l][w][:, k, 128 * o:128 * o + 128],
                                  col[:, l, 2 + k:3 + k], start=(k == 0), stop=(k == 1))
            for dst, l, w in ((psY[:, 0:256], 0, 2), (psY[:, 256:512], 1, 0), (psT[1][:, 0:256], 1, 2)):
                for k in range(2):
                    ins = pe.matmul(dst, col[:, l, 2 + k:3 + k].to_broadcast([128, 128]), W[l][w][:, k, :],
                                    start=(k == 0), stop=(k == 1))
            done.up(ins)
            s_p["film"].wait(pe, 1)
            for l in range(2):
                for o in range(4):
                    c = B * (4 * l + o)
                    for k in range(4):
                        ins = pe.matmul(psT[0][:, c:c + B], EW[:, l, k, 128 * o:128 * o + 128], cT[:, k, :],
                                        start=(k == 0), stop=(k == 3))
            done.up(ins)
            s_p["ve0"].wait(pe, 7)
            s_p["act"].wait(pe, 2)
            s_p["pool"].wait(pe, 1)
            s_p["film"].wait(pe, 21)

            read = []

            def take(*by):
                if read:
                    read[0].wait(pe, *read[1:])
                read[:] = by

            def ctr(n, hf):
                s_mx.wait(pe, n, 8 * hf + 8)
                s_ct.up(pe.transpose(psX[0:16, 0:128], cm[n % 2][:, 16 * hf:16 * hf + 16], ident[:, :]))

            def slot(t, i):
                rowmax(t - 2, 2 * i)
                n = t - 3
                if ok(n):
                    G = 8 * n + i
                    if i == 0:
                        s_in.wait(pe, n)
                        s_cin[0].wait(pe, n)
                    if i == 4:
                        s_cin[1].wait(pe, n)
                    if G >= 2:
                        pe.wait_ge(s_ex.sem, G - 1)
                    for hh in range(2):
                        h = 2 * i + hh
                        for m in range(2):
                            ins = pe.matmul(psT[G % 2][:, 512 * hh + 256 * m:512 * hh + 256 * m + 256],
                                            Ks[n % 3][0:KS, h, 128 * m:128 * m + 128], Qs[n % 3][0:KS, h, :],
                                            start=True, stop=True)
                    s_sT.up(ins)
                if i % 2 == 0:
                    n, gr = (t - 3, i // 2 - 1) if i else (t - 4, 3)
                    if ok(n):
                        s_ex.wait(pe, n, 2 * gr + 2)
                        s_v.wait(pe, n)
                        if 4 * n + gr:
                            pe.wait_ge(s_ye.sem, 4 * n + gr)
                        for m in range(2):
                            for j in range(4):
                                Pj = P[(8 * n + 2 * gr + j // 2) % 4]
                                c0 = 512 * (j % 2) + 256 * m
                                ins = pe.matmul(psY[32 * j:32 * j + 32, 0:T], Vp[n % 4][:, m, 4 * gr + j, :],
                                                Pj[:, c0:c0 + 256], start=(m == 0), stop=(m == 1))
                        s_pv.up(ins)
                rest(t, i)
                rowmax(t - 2, 2 * i + 1)

            def rowmax(n, h):
                if ok(n):
                    if h == 0:
                        s_in.wait(pe, n)
                    if H * n + h >= 2:
                        pe.wait_ge(s_mx.sem, H * n + h - 1)
                    for k in range(2):
                        ins = pe.matmul(psM[h % 2][:, 256 * k:256 * k + 256],
                                        Qs[n % 3][0:KM, h, 128 * k:128 * k + 128], Ks[n % 3][0:KM, h, :],
                                        start=True, stop=True)
                    s_sm.up(ins)

            def rest(t, i):
                if i == 0 and ok(t - 3):
                    take(s_cs, t - 3, 6)
                    ctr(t - 3, 1)
                if i in (1, 2) and ok(t - 4):
                    n, k = t - 4, i - 1
                    s_ye.wait(pe, n)
                    take(s_yd, n, 4 * k + 2)
                    for q in range(4):
                        ins = pe.transpose(psX[:, 128 * q:128 * q + 128], yT[:, q, 128 * k:128 * k + 128], ident[:, :])
                    s_yt.up(ins)
                if i == 3 and ok(t):
                    s_xn.wait(pe, t)
                    take(s_xT, t, 1)
                    for d in range(2):
                        for k in range(2):
                            ins = pe.transpose(psX[:, 256 * d + 128 * k:256 * d + 128 * k + 128],
                                               xn[:, k, 128 * d:128 * d + 128], ident[:, :])
                    s_xtr.up(ins)
                if i in (4, 6) and ok(t):
                    w = (i - 4) // 2
                    s_xT.wait(pe, t)
                    take(s_qf, t, w + 1)
                    for o in range(2):
                        for k in range(2):
                            ins = pe.matmul(psX[:, 256 * o:256 * o + 256], W[0][w][:, k, 128 * o:128 * o + 128],
                                            xT[:, k, :], start=(k == 0), stop=(k == 1))
                    s_qm.up(ins)
                if i == 5 and ok(t - 2):
                    take(s_cs, t - 2, 2)
                    ctr(t - 2, 0)
                if i == 7 and ok(t):
                    take(s_vt, t, 1)
                    for k in range(2):
                        for d in range(2):
                            ins = pe.matmul(psX[:, 256 * k:256 * k + 256], xT[:, d, 128 * k:128 * k + 128],
                                            W[0][2][:, d, :], start=(d == 0), stop=(d == 1))
                    s_vm.up(ins)
            each(slot)
            phase2_pe(pe)


def layer(inputs, l, names):
    return [inputs[f"L{l}_cond_{n}"] for n in names.split()]


def by_d(arrays):
    return [np.moveaxis(np.asarray(a).reshape(*a.shape[:-1], 8, 2, DH), -3, -1).reshape(a.shape) for a in arrays]


def packed(inputs):
    w = [by_d(layer(inputs, 0, "q_w k_w")) + layer(inputs, 0, "v_w out_w"), layer(inputs, 1, "Wq Wk Wv film_out_W")]
    w = np.stack([np.stack([np.asarray(a).reshape(2, 128, D) for a in ws]) for ws in w])
    e = np.stack([np.asarray(layer(inputs, 0, "emb_w")[0]), np.asarray(layer(inputs, 1, "film_emb_W")[0])])
    c = [layer(inputs, 0, "norm_w norm_b") + by_d(layer(inputs, 0, "q_b k_b"))
         + layer(inputs, 0, "emb_b sb_norm_w sb_norm_b"),
         layer(inputs, 1, "norm_scale norm_bias bq bk film_emb_b film_norm_scale film_norm_bias")]
    c = np.stack([np.concatenate([np.asarray(a).reshape(-1, 128) for a in cs]) for cs in c])
    r = np.stack([np.asarray(a) for a in layer(inputs, 0, "v_b out_b") + layer(inputs, 1, "bq bv film_out_b")])
    return {
        "weights": np.ascontiguousarray(w.transpose(3, 0, 1, 2, 4)),
        "emb": np.ascontiguousarray(e.reshape(2, 4, 128, 2 * D).transpose(2, 0, 1, 3)),
        "cols": np.ascontiguousarray(c.transpose(2, 0, 1)),
        "rows": r,
        "ident": np.eye(128, dtype=np.float32),
        "diag": np.kron(np.eye(128 // DH, dtype=np.float32), np.ones((DH, DH), np.float32)),
    }


def kernel(**inputs):
    import concourse.bacc as bacc
    from concourse.bass_utils import run_bass_kernel_spmd

    nc = bacc.Bacc("TRN2", target_bir_lowering=False, num_devices=1)
    given = {
        "x": inputs["x"], "cond": inputs["cond_2048"], "mask_f": inputs["mask_BxS_ff1"],
        "mask_i": inputs["mask_BxS_ik0"],
    }
    arrays, args = {}, []
    for name, a in (given | packed(inputs)).items():
        a = np.ascontiguousarray(a)
        arrays[f"in_{name}"] = a
        args.append(nc.dram_tensor(f"in_{name}", a.shape, mybir.dt.from_np(a.dtype), kind="ExternalInput").ap())
    args.append(nc.dram_tensor("out_0", (B, T, D), F32, kind="ExternalOutput").ap())
    bass_cond_seq_kernel(nc, *args)
    r = run_bass_kernel_spmd(nc, [arrays], core_ids=[0])
    return r.results[0]["out_0"]
```

```python
from contextlib import ExitStack

import numpy as np

import concourse.bass as bass
from concourse import mybir

F32 = mybir.dt.float32
F32R = mybir.dt.float32r
BF16 = mybir.dt.bfloat16
I32 = mybir.dt.int32
ALU = mybir.AluOpType
ACT = mybir.ActivationFunctionType
AX = mybir.AxisListType

B = 32
T = 256
D = 256
H = 16
DH = 16
E = 512
EPS = 1e-5
NEG = -1.0e30
ONES = 0x3F803F80
KM = 99
KS = 102
HB = (0, 10, 16)
HR = (20, 12)


class Count:

    def __init__(self, sem, per=1):
        self.sem, self.per = sem, per

    def up(self, ins):
        ins.then_inc(self.sem, 1)

    def wait(self, eng, n, k=None):
        if n >= 0:
            eng.wait_ge(self.sem, self.per * n + (self.per if k is None else k))


class Landed:

    def __init__(self, sems, per=1):
        self.sems, self.per = sems, per

    def up(self, ins, n):
        ins.then_inc(self.sems[n % len(self.sems)], 16)

    def wait(self, eng, n):
        if n >= 0:
            eng.wait_ge(self.sems[n % len(self.sems)], 16 * self.per * (n // len(self.sems) + 1))


def bass_cond_seq_kernel(nc, x, cond, mask_f, mask_i, weights, emb, cols, rows, ident_d, diag_d, out):
    qd = nc.dram_tensor("q_parts", (B, 3 * DH, H * T), BF16, kind="Internal").ap()
    kd = nc.dram_tensor("k_parts", (B, 3 * DH, H * T), BF16, kind="Internal").ap()
    md = nc.dram_tensor("mask_parts", (B, 3, T), BF16, kind="Internal").ap()

    nd = nc.dram_tensor("key_mask", (B, T), F32, kind="Internal").ap()

    with ExitStack() as ctx:
        def sb(name, shape, dt=F32, scope=ctx):
            return scope.enter_context(nc.sbuf_tensor("sb_" + name, shape, dt))

        def sem(name):
            return ctx.enter_context(nc.semaphore(name))

        def count(name, per=1):
            return Count(sem(name), per)

        def landed(name, ring, per=1):
            return Landed([sem(f"{name}{i}") for i in range(ring)], per)

        psT = [ctx.enter_context(nc.psum_tensor(f"psT{i}", [128, 1024], F32)) for i in range(2)]
        psM = [ctx.enter_context(nc.psum_tensor(f"psM{i}", [128, 512], F32)) for i in range(2)]
        psY = ctx.enter_context(nc.psum_tensor("psY", [128, 512], F32))
        psX = ctx.enter_context(nc.psum_tensor("psX", [128, 512], F32))

        Y = sb("Y", [128, max(2 * B, 34), D])
        Wo = [sb(f"Wo{l}", [128, 2, D]) for l in range(2)]
        W0h, W0l = sb("W0h", [128, 3, 2, D]), sb("W0l", [128, 3, 2, D])
        W0 = Y[:, 28:34, :].rearrange("p (n k) t -> p n k t", n=3)
        EW = Y[:, 0:16, :].rearrange("p (l k a) n -> p l k (a n)", l=2, k=4)
        Qs = [sb(f"Qs{i}", [128, H, T], BF16) for i in range(3)]
        Ks = [sb(f"Ks{i}", [128, H, T], BF16) for i in range(3)]
        P = [sb(f"P{i}", [128, 1024]) for i in range(4)]
        Vp = [sb(f"Vp{i}", [128, 2, H, 32]) for i in range(3)]
        ident = sb("ident", [128, 128])
        xn = sb("xn", [128, 2, D])
        xT = sb("xT", [128, 2, T])
        qp = [sb(f"qp{i}", [128, 3, 2, T], BF16) for i in range(2)]
        yT = sb("yT", [128, 4, T])
        yr = sb("yr", [128, 2, D])
        rb = sb("rb", [128, 5, D])
        vb0, ob0, qb1, vb1, ob1 = (rb[:, r:r + 1, :].to_broadcast([128, 2, D]) for r in range(5))
        cm = [sb(f"cm{i}", [128, 2 * H]) for i in range(2)]
        cp = [sb(f"cp{i}", [HR[i], 3, 128], BF16) for i in range(2)]
        cr = sb("cr", [HR[0], 128])
        st = sb("st", [128, 4, 6])
        mv = sb("mv", [128, 4, 2])
        ve = sb("ve", [128, 4])
        rs = sb("rs", [128, 4])
        nm = sb("nm", [128, 4])
        rd = sb("rd", [128, H])
        rd2 = sb("rd2", [128, 2, 2, 8])
        xT2 = sb("xT2", [128, 2, T])
        xT1 = [xT[:, :, :], xT2[:, :, :]]
        ph = sb("ph", [128, 2])
        bq = sb("bq", [128, 6])
        col = sb("col", [128, 2, 16])
        cT = sb("cT", [128, 4, B])
        cond_sb = Y[0:B, 16:18, :].rearrange("b a n -> b (a n)")
        tc = Y[:, 18, 0:4 * B].rearrange("p (k b) -> p k b", k=4)
        sc = Y[:, 19, 0:4 * B].rearrange("p (l d b) -> p l d b", l=2, d=2)
        FA = sb("FA", [128, 2, 2, B])
        FB = sb("FB", [128, 2, 2, B])
        kT = sb("kT", [128, 2, B])
        mrow, mr2, mr3, keep = (Y[0:B, n, :] for n in range(20, 24))
        irow = Y[0:B, 24, :].bitcast(I32)
        mp = Y[0:B, 26:28, :].rearrange("b a n -> b (a n)").bitcast(BF16)[:, 0:3 * T].rearrange("b (c t) -> b c t", c=3)
        mT = sb("mT", [128, 2, B])
        diag = sb("diag", [128, 128])
        BD = sb("BD", [128, 4, 136])
        qm = sb("qm", [128, 2 * H])
        kx = sb("kx", [128, 2])
        ksum = sb("ksum", [128, 2])
        kd2 = sb("kd2", [128, 2])
        with ExitStack() as own:
            xt = [sb(f"xt{i}", [128, 2, D], scope=own) for i in range(2)]
            qf = [sb(f"qf{i}", [128, 2, T], scope=own) for i in range(2)]
            rf = sb("rf", [128, 2, T], scope=own)
            vt = sb("vt", [128, 2, D], scope=own)
            W1 = sb("W1", [128, 3, 2, D], scope=own)
        W1h, W1l = sb("W1h", [128, 3, 2, D]), sb("W1l", [128, 3, 2, D])
        xTl = [sb(f"xTl{i}", [128, 2, T]) for i in range(2)]
        W = [[(W0, W1)[l][:, n, :, :] for n in range(3)] + [Wo[l][:, :, :]] for l in range(2)]

        s_ld = [sem(f"s_ld{i}") for i in range(3)]
        s_x = landed("s_x", 2)
        s_st = count("s_st", 4)
        s_rs = count("s_rs", 4)
        s_xn = count("s_xn")
        s_xtr = count("s_xtr")
        s_xT = count("s_xT")
        s_xl = count("s_xl")
        s_w0 = count("s_w0", 2)
        s_w1 = count("s_w1", 2)
        s_qm = count("s_qm", 2)
        s_qf = count("s_qf", 2)
        s_hi = count("s_hi", 2)
        s_rf = count("s_rf", 2)
        s_mi = count("s_mi", 2)
        s_lo = count("s_lo", 2)
        s_qo = [landed("s_qo", 2), landed("s_ko", 2)]
        s_in = landed("s_in", 3, 7)
        s_vm = count("s_vm")
        s_vt = count("s_vt")
        s_v = count("s_v")
        s_sm = count("s_sm", H)
        s_mx = count("s_mx", H)
        s_ct = count("s_ct", 2)
        s_cs = count("s_cs", 8)
        s_cin = [landed("s_ca", 2, 3), landed("s_cb", 2, 3)]
        s_sT = count("s_sT", 8)
        s_ex = count("s_ex", 8)
        s_pv = count("s_pv", 4)
        s_ye = count("s_ye", 4)
        s_yt = count("s_yt", 2)
        s_yd = count("s_yd", 8)
        s_yr = count("s_yr", 4)
        s_y = count("s_y", 2)

        block = ctx.enter_context(nc.Block())
        LOADS = (3, 3, 6)

        def loaded(eng, i):
            eng.wait_ge(s_ld[i], 16 * LOADS[i])

        def each(fn, run):
            for t in range(B + 4):
                for i in range(8):
                    if (t, i) in EARLY:
                        run(EARLY[t, i])
                    fn(t, i)

        def ok(n):
            return 0 <= n < B

        s_p = {k: count("p_" + k) for k in ("ve0", "pe", "act", "pool", "mneg", "film")}
        s_md = landed("s_md", 1, 2)

        PE = ((0, "f0"), (1, "o0"), (2, "k"), (2, "q"), (2, "v"), (3, "kv"), (4, "f1"), (5, "o1"), (3, "y"), (1,
              "tr"), (2, "kt"), (2, "qt"))
        AC = ((3, "kn"), (0, "u0"), (0, "t0"), (3, "qe"), (5, "t1"), (4, "yn"), (1, "xn"), (2, "ke"), (2, "vk"),
              (4, "u1"), (1, "xT"))
        DV = ((4, "st1"), (1, "x1"), (0, "h0"), (1, "st0"), (2, "dk"), (2, "dq"), (5, "h1"), (2, "mk"), (2, "mq"),
              (2, "dv"), (3, "bd"), (2, "ken"), (5, "ob"), (3, "yd"), (1, "xl"))
        GP = ((0, "xb"), (4, "rs1"), (1, "rs0"), (1, "xo"), (2, "qs"))
        ROUNDS = B + 5
        room = [r[:, :, :].rearrange("p h t -> p (h t)").bitcast(F32)[:, 512 * u:512 * u + 512]
                for b in range(B - 3, B) for r in (Qs[b % 3], Ks[b % 3]) for u in range(4)]
        room += [r[:, 512 * u:512 * u + 512] for r in P for u in range(2)]
        room += [r[:, u, :, :].rearrange("p h d -> p (h d)") for r in Vp for u in range(2)]

        room += [yT[:, u:u + 2, :].rearrange("p q t -> p (q t)") for u in (0, 2)]

        def unit():
            return room.pop(0).rearrange("p (k t) -> p k t", k=2)

        xr = [unit() for _ in range(3)]
        xb = [unit() for _ in range(2)]
        ub, th, hb = ([[unit() for _ in range(2)] for _ in range(2)] for _ in range(3))
        kr = [unit() for _ in range(2)]
        x1 = [unit() for _ in range(6)]
        km, ke, ken, v1, ob = (unit() for _ in range(5))
        tq, kn, vk, qe, yn = ([unit() for _ in range(2)] for _ in range(5))
        R = [psT[0][:, 0:512], psT[0][:, 512:1024], psT[1][:, 0:512], psT[1][:, 512:1024],
             psM[0][:, :], psM[1][:, :], psY[:, :], psX[:, :]]
        BANK = {"v": 0, "qt": 2, "f1": 3, "k": 7, "o1": 4, "o0": 3, "q": 2, "kv": 7, "f0": 4, "kt": 5, "tr": 6}

        def tiles(step):
            return R[BANK[step]].rearrange("p (k t) -> p k t", k=2)

        e = {name: count("e_" + name, {"st0": 4, "st1": 4, "rs0": 4, "rs1": 4, "yd": 2, "ken": 2}.get(name, 1))
             for order in (PE, AC, DV, GP) for _, name in order}
        e_xr = landed("e_xr", 3)
        e_kr = landed("e_kr", 2)
        e_out = landed("e_out", 1)

        EARLY = {(B + 2, 4): 0, (B + 3, 3): 1, (B + 3, 5): 2}

        def freed(eng, t):
            if t == 0:
                s_sT.wait(eng, B - 2)
            if t == 1:
                s_sT.wait(eng, B - 1)
            if t == 2:
                s_pv.wait(eng, B - 1)
            if t == 3:
                s_y.wait(eng, B - 1)

        def rounds(eng, steps, order):
            def run(t):
                freed(eng, t)
                for lag, name in order:
                    if 0 <= t - lag < B:
                        steps[name](t - lag)
            return run

        def late(run):
            for t in range(len(EARLY), ROUNDS):
                run(t)

        def phase2_sp(sp):
            freed(sp, 0)

            def load(n):
                if n < B:
                    e["xb"].wait(sp, n - 3)
                    e_xr.up(sp.dma_start(xr[n % 3], x[n].rearrange("(k p) d -> p k d", p=128)), n)
            load(0)
            load(1)
            for t in range(ROUNDS):
                if t:
                    freed(sp, t)
                load(t + 2)
                if t >= 1 and t - 1 < B:
                    n = t - 1
                    e["dk"].wait(sp, n - 2)
                    e_kr.up(sp.dma_start(kr[n % 2][:, 0, :], nd[n:n + 1, :].to_broadcast([128, T])), n)
                if t >= 5:
                    n = t - 5
                    e["ob"].wait(sp, n)
                    e_out.up(sp.dma_start(out[n].rearrange("(k p) d -> p k d", p=128), ob), n)
            e_out.wait(sp, B - 1)

        def phase2_gpsimd(g):

            def xb_(n):
                e_xr.wait(g, n)
                e["x1"].wait(g, n - 2)
                e["xb"].up(g.tensor_tensor(xb[n % 2], xr[n % 3], ob0, ALU.add))

            def xo_(n):
                e["xn"].wait(g, n)
                e["xo"].up(g.tensor_tensor(x1[n % 6], x1[n % 6], ob1, ALU.add))

            def rs_(l, used):
                def f(n):
                    k, sig = slice(2 * l, 2 * l + 2), e[f"rs{l}"]
                    e[f"st{l}"].wait(g, n)
                    e[used].wait(g, n - 1)
                    sig.up(g.tensor_scalar(ve[:, k], mv[:, k, 1], EPS, None, ALU.add))
                    sig.wait(g, n, 1)
                    sig.up(g.tensor_tensor(rs[:, k], ve[:, k], ph[:, :], ALU.pow))
                    sig.wait(g, n, 2)
                    sig.up(g.tensor_tensor(ve[:, k], mv[:, k, 0], rs[:, k], ALU.mult))
                    sig.wait(g, n, 3)
                    sig.up(g.tensor_scalar(nm[:, k], ve[:, k], -1.0, None, ALU.mult))
                return f

            def qs_(n):
                e["mq"].wait(g, n)
                q4 = tq[n % 2].rearrange("p k (h d) -> p (k h) d", d=DH)
                e["qs"].up(g.tensor_tensor(
                    q4, q4, qm[:, :].rearrange("p (h a) -> p h a", a=1).to_broadcast([128, 2 * H, DH]), ALU.add))
            return rounds(g, {"xb": xb_, "xo": xo_, "rs0": rs_(0, "xn"), "rs1": rs_(1, "yn"), "qs": qs_}, GP)

        def phase2_act(a):

            def u_(l):
                def f(n):
                    e[f"f{l}"].wait(a, n)
                    e[f"h{l}"].wait(a, n - 2)
                    for d in range(2):
                        ins = a.activation(ub[l][n % 2][:, d, :], tiles(f"f{l}")[:, d, :], ACT.Identity,
                                           bias=FB[:, l, d, n:n + 1], scale=FA[:, l, d, n:n + 1])
                    e[f"u{l}"].up(ins)
                return f

            def t_(l):
                def f(n):
                    e[f"u{l}"].wait(a, n)
                    e[f"h{l}"].wait(a, n - 2)
                    e[f"t{l}"].up(a.activation(th[l][n % 2], ub[l][n % 2], ACT.Tanh))
                return f

            def xn_(n):
                e["rs0"].wait(a, n)
                e["tr"].wait(a, n - 1)
                for i in range(2):
                    ins = a.activation(xn[:, i, :], x1[n % 6][:, i, :], ACT.Identity, bias=nm[:, i:i + 1],
                                       scale=rs[:, i:i + 1])
                e["xn"].up(ins)

            def yn_(n):
                e["rs1"].wait(a, n)
                e["f1"].wait(a, n - 2)
                for i in range(2):
                    ins = a.activation(yn[n % 2][:, i, :], yr[:, i, :], ACT.Identity, bias=nm[:, 2 + i:3 + i],
                                       scale=rs[:, 2 + i:3 + i])
                e["yn"].up(ins)

            def xT_(n):
                e["tr"].wait(a, n)
                for s in "qkv":
                    e[s].wait(a, n - 2)
                e["xT"].up(a.activation(xT1[n % 2].bitcast(F32R), tiles("tr"), ACT.Identity))

            def ke_(n):
                e["mk"].wait(a, n)
                e["ken"].wait(a, n - 1)
                for i in range(2):
                    ins = a.activation(ke[:, i, :], km[:, i, :], ACT.Exp, bias=kx[:, i:i + 1],
                                       accum_out=ksum[:, i:i + 1])
                e["ke"].up(ins)

            def vk_(n):
                e["dv"].wait(a, n)
                e["kv"].wait(a, n - 2)
                for i in range(2):
                    ins = a.activation(vk[n % 2][:, i, :], v1[:, i, :], ACT.Identity, scale=kT[:, i, n:n + 1])
                e["vk"].up(ins)

            def qe_(n):
                e["qt"].wait(a, n)
                e["y"].wait(a, n - 2)
                e["qe"].up(a.activation(qe[n % 2], tiles("qt"), ACT.Exp))

            def kn_(n):
                e["kt"].wait(a, n)
                e["kv"].wait(a, n - 2)
                e["kn"].up(a.activation(kn[n % 2], tiles("kt"), ACT.Identity))
            return rounds(a, {"u0": u_(0), "u1": u_(1), "t0": t_(0), "t1": t_(1), "xn": xn_, "yn": yn_, "xT": xT_, "ke": ke_,
                    "vk": vk_, "qe": qe_, "kn": kn_}, AC)

        def phase2_dve(v):

            def h_(l):
                def f(n):
                    e[f"t{l}"].wait(v, n)
                    e[f"o{l}"].wait(v, n - 2)
                    e[f"h{l}"].up(v.scalar_tensor_tensor(hb[l][n % 2], th[l][n % 2], 1.0, ub[l][n % 2],
                                                         ALU.add, ALU.mult))
                return f

            def x1_(n):
                e["o0"].wait(v, n)
                e["xb"].wait(v, n)
                e["ob"].wait(v, n - 6)
                e["x1"].up(v.tensor_tensor(x1[n % 6], tiles("o0"), xb[n % 2], ALU.add))

            def st_(l, src, after, used):
                def f(n):
                    e[after].wait(v, n)
                    e[used].wait(v, n - 1)
                    for i in range(2):
                        e[f"st{l}"].up(v.bn_stats(st[:, 2 * l + i, :], src(n)[:, i, :]))
                    for i in range(2):
                        e[f"st{l}"].wait(v, n, 1 + i)
                        e[f"st{l}"].up(v.bn_aggr(mv[:, 2 * l + i, :], st[:, 2 * l + i, :]))
                return f

            def xl_(n):
                e["xT"].wait(v, n)
                for s in "qkv":
                    e[s].wait(v, n - 2)
                e["xl"].up(v.tensor_tensor(xTl[n % 2][:, :, :].bitcast(F32R), tiles("tr"), xT1[n % 2], ALU.subtract))

            def dq_(n):
                e["q"].wait(v, n)
                e["qt"].wait(v, n - 2)
                e["dq"].up(v.tensor_tensor(tq[n % 2], tiles("q"), qb1, ALU.add))

            def mq_(n):
                e["dq"].wait(v, n)
                e["qs"].wait(v, n - 1)
                e["mq"].up(v.tensor_reduce(qm[:, :], tq[n % 2].rearrange("p k (h d) -> p (k h) d", d=DH), AX.X,
                                           ALU.max, negate=True))

            def dk_(n):
                e["k"].wait(v, n)
                e_kr.wait(v, n)
                e["ke"].wait(v, n - 1)
                for i in range(2):
                    ins = v.scalar_tensor_tensor(km[:, i, :], tiles("k")[:, i, :], bq[:, 4 + i:5 + i],
                                                 kr[n % 2][:, 0, :], ALU.add, ALU.add)
                e["dk"].up(ins)

            def mk_(n):
                e["dk"].wait(v, n)
                e["ke"].wait(v, n - 1)
                e["mk"].up(v.tensor_reduce(kx[:, :], km, AX.X, ALU.max, negate=True))

            def ken_(n):
                e["ke"].wait(v, n)
                e["kt"].wait(v, n - 1)
                e["ken"].up(v.reciprocal(kd2[:, :], ksum[:, :]))
                e["ken"].wait(v, n, 1)
                for i in range(2):
                    ins = v.tensor_scalar(ken[:, i, :], ke[:, i, :], kd2[:, i:i + 1], None, ALU.mult)
                e["ken"].up(ins)

            def dv_(n):
                e["v"].wait(v, n)
                e["vk"].wait(v, n - 1)
                e["dv"].up(v.tensor_tensor(v1, tiles("v"), vb1, ALU.add))

            def bd_(n):
                e["kv"].wait(v, n)
                e["y"].wait(v, n - 2)
                e["bd"].up(v.tensor_tensor(BD[:, 2 * (n % 2):2 * (n % 2) + 2, 0:128], tiles("kv")[:, :, 0:128],
                                           diag[:, :].rearrange("p (a e) -> p a e", a=1).to_broadcast([128, 2, 128]),
                                           ALU.mult))

            def yd_(n):
                e["y"].wait(v, n)
                e["yn"].wait(v, n - 1)
                ps = psT[0][:, :].rearrange("p (i c) -> p i c", i=2)[:, :, 0:272]\
                    .rearrange("p i (f c) -> p i f c", f=2)
                for i in range(2):
                    ins = v.reciprocal(rd2[:, i, :, :], ps[:, i, :, 128:136])
                e["yd"].up(ins)
                e["yd"].wait(v, n, 1)
                for i in range(2):
                    for f in range(2):
                        ins = v.tensor_tensor(
                            yr[:, i, 128 * f:128 * f + 128].rearrange("p (h e) -> p h e", e=DH),
                            ps[:, i, f, 0:128].rearrange("p (h e) -> p h e", e=DH),
                            rd2[:, i, f, :].rearrange("p (h a) -> p h a", a=1).to_broadcast([128, 8, DH]), ALU.mult)
                e["yd"].up(ins)

            def ob_(n):
                e["o1"].wait(v, n)
                e["xo"].wait(v, n)
                e_out.wait(v, n - 1)
                e["ob"].up(v.tensor_tensor(ob, tiles("o1"), x1[n % 6], ALU.add))
            return rounds(v, {"h0": h_(0), "h1": h_(1), "x1": x1_, "st0": st_(0, lambda n: x1[n % 6], "x1", "rs0"),
                    "st1": st_(1, lambda n: yr, "yd", "rs1"), "dq": dq_, "mq": mq_, "dk": dk_, "mk": mk_,
                    "ken": ken_, "dv": dv_, "bd": bd_, "yd": yd_, "ob": ob_, "xl": xl_}, DV)

        def phase2_pe(pe):
            read = {}

            def take(bank, step, n, k=None):
                if bank in read:
                    m = read[bank]
                    e[m[0]].wait(pe, *m[1:])
                read[bank] = (step, n, k)

            def turned(step, n, reader, src):
                take(BANK[step], reader, n)
                for a in range(2):
                    for b in range(2):
                        ins = pe.transpose(tiles(step)[:, a, 128 * b:128 * b + 128],
                                           src[b][:, 128 * a:128 * a + 128], ident[:, :])
                e[step].up(ins)

            def natural(step, n, reader, lhs, w):
                take(BANK[step], reader, n)
                for i in range(2):
                    for d in range(2):
                        ins = pe.matmul(tiles(step)[:, i, :], lhs[:, d, 128 * i:128 * i + 128], w[:, d, :],
                                        start=(d == 0), stop=(d == 1))
                e[step].up(ins)

            def f0_(n):
                if n == 0:
                    s_mx.wait(pe, B - 1)
                s_y.wait(pe, n)
                turned("f0", n, "u0", [Y[:, 2 * n + i, :] for i in range(2)])

            def f1_(n):
                e["yn"].wait(pe, n)
                turned("f1", n, "u1", [yn[n % 2][:, i, :] for i in range(2)])

            def tr_(n):
                if n == 0:
                    s_ye.wait(pe, B - 1)
                e["xn"].wait(pe, n)
                turned("tr", n, "xl", [xn[:, i, :] for i in range(2)])

            def qt_(n):
                e["qs"].wait(pe, n)
                turned("qt", n, "qe", [tq[n % 2][:, i, :] for i in range(2)])

            def kt_(n):
                e["ken"].wait(pe, n)
                turned("kt", n, "kn", [ken[:, i, :] for i in range(2)])

            def o_(l):
                def f(n):
                    if n == 0:
                        s_ex.wait(pe, B - 1)
                    e[f"h{l}"].wait(pe, n)
                    natural(f"o{l}", n, ("x1", "ob")[l], hb[l][n % 2], W[l][3])
                return f

            def qv_(step, reader, w):
                def f(n):
                    e["xl"].wait(pe, n)
                    take(BANK[step], reader, n)
                    for i in range(2):
                        ins = product(pe, tiles(step)[:, i, :], cut((xT1[n % 2], xTl[n % 2]), i),
                                      cut((W1h[:, w, :, :], W1l[:, w, :, :])))
                    e[step].up(ins)
                return f

            def k_(n):
                if n == 0:
                    s_yd.wait(pe, B - 1, 6)
                    s_w1.wait(pe, 0)
                e["xl"].wait(pe, n)
                take(BANK["k"], "dk", n)
                for o in range(2):
                    ins = product(pe, tiles("k")[:, o, :], cut((W1h[:, 1, :, :], W1l[:, 1, :, :]), o), cut((xT1[n % 2], xTl[n % 2])))
                e["k"].up(ins)

            def kv_(n):
                e["kn"].wait(pe, n)
                e["vk"].wait(pe, n)
                take(BANK["kv"], "bd", n)
                for f in range(2):
                    for i in range(2):
                        ins = pe.matmul(tiles("kv")[:, f, 0:128], vk[n % 2][:, i, 128 * f:128 * f + 128],
                                        kn[n % 2][:, i, 128 * f:128 * f + 128], start=(i == 0), stop=(i == 1))
                e["kv"].up(ins)

            def y_(n):
                e["bd"].wait(pe, n)
                e["qe"].wait(pe, n)
                for i in range(2):
                    take(i, "yd", n)
                for i in range(2):
                    for f in range(2):
                        ins = pe.matmul(R[i][:, 136 * f:136 * f + 136], qe[n % 2][:, f, 128 * i:128 * i + 128],
                                        BD[:, 2 * (n % 2) + f, :], start=True, stop=True)
                e["y"].up(ins)
            return rounds(pe, {"f0": f0_, "f1": f1_, "tr": tr_, "qt": qt_, "kt": kt_, "o0": o_(0), "o1": o_(1), "q": qv_("q", "dq", 0),
                    "v": qv_("v", "dv", 2), "k": k_, "kv": kv_, "y": y_}, PE)
        def product(pe, dst, lhs, rhs):
            terms = [(a, b, d) for a, b in ((0, 1), (1, 0), (0, 0)) for d in range(2)]
            for m, (a, b, d) in enumerate(terms):
                ins = pe.matmul(dst, lhs[a](d).bitcast(F32R), rhs[b](d).bitcast(F32R), start=(m == 0), stop=(m == 5))
            return ins

        def cut(pair, k=None):
            return [(lambda d, r=r: r[:, d, :] if k is None else r[:, d, 128 * k:128 * k + 128]) for r in pair]

        SV = 2

        def split(eng, n, w):
            s_qf.wait(eng, n, w + 1)
            s_qo[w].wait(eng, n - 1)
            s_lo.wait(eng, n - 1 + w, 2 - w)
            s_hi.up(eng.tensor_scalar(qp[w][:, 0, :, :], qf[w][:, :, :], 1.0, None, ALU.mult))
            s_hi.wait(eng, n, w + 1)
            s_rf.up(eng.tensor_tensor(rf[:, :, :], qf[w][:, :, :], qp[w][:, 0, :, :], ALU.subtract))
            s_rf.wait(eng, n, w + 1)
            s_mi.up(eng.tensor_scalar(qp[w][:, 1, :, :], rf[:, :, :], 1.0, None, ALU.mult))
            s_mi.wait(eng, n, w + 1)
            s_lo.up(eng.tensor_tensor(qp[w][:, 2, :, :], rf[:, :, :], qp[w][:, 1, :, :], ALU.subtract))

        @block.sync
        def _(sp):
            def load(i, *pairs):
                for dst, src in pairs:
                    sp.dma_start(dst, src).then_inc(s_ld[i], 16)

            def xload(n):
                s_x.up(sp.dma_start(xt[n % 2][:, :, :], x[n].rearrange("(k p) d -> p k d", p=128)), n)
            load(0, (mrow[:, :], mask_f), (irow[:, :], mask_i), (ident[:, :], ident_d))
            xload(0)
            load(1, (col[:, :, :], cols), (W0, weights[:, 0, 0:3]),
                 (rb[:, :, :], rows.rearrange("(a r) n -> a r n", a=1).to_broadcast([128, 5, D])))
            xload(1)
            load(2, (cond_sb, cond), (EW, emb), (W1[:, :, :, :], weights[:, 1, 0:3]),
                 (Wo[0][:, :, :], weights[:, 0, 3]), (Wo[1][:, :, :], weights[:, 1, 3]), (diag[:, :], diag_d))
            s_p["ve0"].wait(sp, 6)
            s_p["pool"].wait(sp, 1)
            s_md.up(sp.dma_start(md.rearrange("b c t -> b (c t)"), mp[:, :, :]), 0)
            s_p["mneg"].wait(sp, 2)
            s_md.up(sp.dma_start(nd, mr3[:, :]), 0)
            s_md.wait(sp, 0)

            def c_in(n, hf):
                s_cs.wait(sp, n, 4 * hf + 4)
                for p in range(3):
                    s_cin[hf].up(sp.dma_start(
                        Qs[n % 3][KM + p:KM + p + 1, HB[hf]:HB[hf + 1], :], cp[hf][:, p, :]), n)

            def parts_out(n, w):
                s_lo.wait(sp, n, w + 1)
                s_qo[w].up(sp.dma_start((qd, kd)[w][n].rearrange("(c d) (h t) -> (d h) c t", c=3, h=8),
                                        qp[w][:, :, :, :].rearrange("p c o t -> p c (o t)")), n)

            def parts_in(n):
                s_qo[0].wait(sp, n)
                s_qo[1].wait(sp, n)
                s_sT.wait(sp, n - 3)
                for r, c, w in ((0, 0, 3), (48, 1, 2), (80, 2, 1)):
                    s_in.up(sp.dma_start(Qs[n % 3][r:r + 16 * w, :, :].rearrange("p h t -> p (h t)"),
                                         qd[n, 0:16 * w]), n)
                    s_in.up(sp.dma_start(
                        Ks[n % 3][r:r + 16 * w, :, :].rearrange("p h t -> p (h t)"),
                        kd[n, 16 * c:16 * c + 16].rearrange("(a d) t -> a d t", a=1).to_broadcast([w, DH, H * T])), n)
                s_in.up(sp.dma_start(Ks[n % 3][96:99, :, :],
                                     md[n].rearrange("c (a t) -> c a t", a=1).to_broadcast([3, H, T])), n)

            for t in range(B + 4):
                if ok(t + 2):
                    s_xn.wait(sp, t)
                    xload(t + 2)
                if ok(t - 3):
                    c_in(t - 3, 1)
                if ok(t - 1):
                    parts_in(t - 1)
                if ok(t - 2):
                    c_in(t - 2, 0)
                if ok(t):
                    parts_out(t, 0)
                    parts_out(t, 1)
            phase2_sp(sp)

        @block.gpsimd
        def _(g):
            z = s_p["pool"]
            z.up(g.memset(ph[:, :], -0.5))
            z.wait(g, 0)
            for i in range(3):
                ins = g.memset(Ks[i][96:KS, :, :].bitcast(I32), ONES)
            z.up(ins)

            def rstd(c, n, k, sig, m):
                sig.up(g.tensor_scalar(ve[:, k], mv[:, k, 1], EPS, None, ALU.add))
                sig.wait(g, n, m + 1)
                sig.up(g.tensor_tensor(rs[:, k], ve[:, k], ph[:, c], ALU.pow))
                sig.wait(g, n, m + 2)
                sig.up(g.tensor_tensor(ve[:, k], mv[:, k, 0], rs[:, k], ALU.mult))
                sig.wait(g, n, m + 3)
                sig.up(g.tensor_scalar(nm[:, k], ve[:, k], -1.0, None, ALU.mult))

            def norm0(n):
                s_st.wait(g, n)
                s_xn.wait(g, n - 1)
                rstd(slice(0, 2), n, slice(0, 2), s_rs, 0)

            z.wait(g, 1)
            norm0(0)
            s_rs.wait(g, 0)
            for i in range(3):
                ins = g.memset(Vp[i][:, :, :, 17:32], 0.0)
                ins = g.memset(Vp[i][:, :, :, 16:17], 1.0)
            z.up(ins)
            z.wait(g, 2)

            run = phase2_gpsimd(g)

            def slot(t, i):
                if i == 4 and ok(t + 1):
                    norm0(t + 1)
                if i == 4 and ok(t - 4):
                    n = t - 4
                    s_yd.wait(g, n)
                    s_y.wait(g, n - 1)
                    rstd(slice(0, 2), n, slice(2, 4), s_yr, 0)
                if i in (4, 6) and t >= SV and ok(t):
                    split(g, t, (i - 4) // 2)
            each(slot, run)
            late(run)

        @block.scalar
        def _(a):
            done = s_p["act"]
            s_p["pe"].wait(a, 0)
            for k, dst in enumerate((mT, kT)):
                ins = a.activation(dst[:, :, :], psX[:, 2 * B * k:2 * B * k + 2 * B].rearrange("p (k b) -> p k b", k=2),
                                   ACT.Identity)
            done.up(ins)
            done.wait(a, 0)

            def through(*to):
                for n, l, w in to:
                    for o in range(2):
                        c = 2 * n + o
                        ins = a.activation(bq[:, c:c + 1], psM[0][:, c:c + 1], ACT.Identity,
                                           bias=col[:, l, 4 + 2 * w + o:5 + 2 * w + o])
                done.up(ins)

            def xnorm(n):
                s_rs.wait(a, n)
                s_xtr.wait(a, n - 1)
                for k in range(2):
                    ins = a.activation(xn[:, k, :], xt[n % 2][:, k, :], ACT.Identity, bias=nm[:, k:k + 1],
                                       scale=rs[:, k:k + 1])
                s_xn.up(ins)

            xnorm(0)
            s_p["pe"].wait(a, 1)
            loaded(a, 1)
            through((0, 0, 0), (1, 0, 1))
            done.wait(a, 1)

            run = phase2_act(a)

            def slot(t, i):
                if (t, i) == (0, 7):
                    s_p["pe"].wait(a, 2)
                    done.up(a.activation(tc, psM[1][:, 0:4 * B].rearrange("p (k b) -> p k b", k=4), ACT.Tanh,
                                         scale=0.5))
                if (t, i) == (1, 3):
                    s_p["pe"].wait(a, 3)
                    through((2, 1, 1))
                    done.wait(a, 3)
                if ok(t - 3):
                    n = t - 3
                    G = 8 * n + i
                    s_sT.wait(a, n, i + 1)
                    if G >= 4:
                        a.wait_ge(s_pv.sem, (G - 4) // 2 + 1)
                    s_ex.up(a.activation(P[G % 4][:, :], psT[G % 2][:, :], ACT.Exp))
                if i == 1 and ok(t):
                    s_xtr.wait(a, t)
                    s_vm.wait(a, t - 1)
                    s_xT.up(a.activation(xT[:, :, :].bitcast(F32R), psX[:, :].rearrange("p (k t) -> p k t", k=2), ACT.Identity))
                if i % 2:
                    n, gr = (t - 3, i // 2 - 1) if i > 1 else (t - 4, 3)
                    if ok(n):
                        s_pv.wait(a, n, gr + 1)
                        s_yt.wait(a, n - 1)
                        s_ye.up(a.activation(yT[:, gr, :], psY[:, 0:T], ACT.Identity))
                if i == 7 and ok(t + 1):
                    xnorm(t + 1)
                if i == 5 and ok(t - 1):
                    n = t - 1
                    s_vt.wait(a, n)
                    s_pv.wait(a, n - 3)
                    for k in range(2):
                        ins = a.activation(Vp[n % 3][:, k, :, 0:16],
                                           vt[:, k, :].rearrange("p (h d) -> p h d", d=DH), ACT.Identity,
                                           scale=mT[:, k, n:n + 1])
                    s_v.up(ins)
                if i in (4, 6) and ok(t):
                    w = (i - 4) // 2
                    s_qm.wait(a, t, w + 1)
                    s_rf.wait(a, t - 1, w + 1)
                    for o in range(2):
                        ins = a.activation(qf[w][:, o, :], psX[:, T * o:T * o + T], ACT.Identity,
                                           bias=bq[:, 2 * w + o:2 * w + o + 1])
                    s_qf.up(ins)
                if i in (6, 7) and ok(t - 4):
                    n, k = t - 4, i - 6
                    s_yr.wait(a, n)
                    if n == 0:
                        s_p["film"].wait(a, 21)
                        s_md.wait(a, 0)
                    s_y.up(a.activation(Y[:, 2 * n + k, :], yr[:, k, :], ACT.Identity, bias=nm[:, 2 + k:3 + k],
                                        scale=rs[:, 2 + k:3 + k]))
            each(slot, run)
            late(run)

        @block.vector
        def _(v):
            z = s_p["ve0"]
            for i in range(3):
                ins = v.memset(Qs[i][96:KS, :, :].bitcast(I32), ONES)
            z.up(ins)
            loaded(v, 0)
            y = s_p["mneg"]
            y.up(v.tensor_scalar(mr3[:, :], irow[:, :], 1, None, ALU.is_equal))
            y.wait(v, 0)
            y.up(v.tensor_scalar(keep[:, :], mr3[:, :], -1.0, 1.0, ALU.mult, ALU.add))
            y.wait(v, 1)
            y.up(v.tensor_scalar(mr3[:, :], mr3[:, :], NEG, None, ALU.mult))
            z.up(v.tensor_scalar(mr2[:, :], mrow[:, :], -1.0, 1.0, ALU.mult, ALU.add))
            z.wait(v, 1)
            z.up(v.tensor_scalar(mr2[:, :], mr2[:, :], -1000000.0, None, ALU.mult))
            z.wait(v, 2)
            z.up(v.tensor_copy(mp[:, 0, :], mr2[:, :]))
            z.wait(v, 3)
            z.up(v.tensor_tensor(mr2[:, :], mr2[:, :], mp[:, 0, :], ALU.subtract))
            z.wait(v, 4)
            z.up(v.tensor_copy(mp[:, 1, :], mr2[:, :]))
            z.wait(v, 5)
            z.up(v.tensor_tensor(mp[:, 2, :], mr2[:, :], mp[:, 1, :], ALU.subtract))
            def stats(n):
                s_x.wait(v, n)
                s_xn.wait(v, n - 1)
                for k in range(2):
                    s_st.up(v.bn_stats(st[:, k, :], xt[n % 2][:, k, :]))
                for k in range(2):
                    s_st.wait(v, n, k + 1)
                    s_st.up(v.bn_aggr(mv[:, k, :], st[:, k, :]))

            stats(0)

            def scaled(l):
                for n in range(3):
                    for k in range(2):
                        ins = v.tensor_scalar(W[l][n][:, k, :], W[l][n][:, k, :], col[:, l, k:k + 1], None, ALU.mult)
                z.up(ins)

            def parted(sig, w, hi, lo):
                sig.up(v.tensor_copy(hi[:, :, :, :].bitcast(F32R), w))
                sig.wait(v, 0, 1)
                for m in (slice(0, 2), slice(2, 3)):
                    ins = v.tensor_tensor(lo[:, m, :, :].bitcast(F32R), w[:, m, :, :], hi[:, m, :, :], ALU.subtract)
                sig.up(ins)

            loaded(v, 1)
            s_p["pe"].wait(v, 1)
            v.tensor_tensor(rb[:, 0, :], rb[:, 0, :], psY[:, 0:256], ALU.add)
            scaled(0)
            z.wait(v, 7)
            parted(s_w0, W0, W0h, W0l)

            def silu():
                y = s_p["film"]
                s_p["act"].wait(v, 2)
                y.up(v.scalar_tensor_tensor(cT[:, :, :], tc, 1.0, psM[1][:, 0:4 * B].rearrange("p (k b) -> p k b", k=4),
                                            ALU.add, ALU.mult))
                y.wait(v, 0)
                y.up(v.tensor_scalar(cT[:, :, :], cT[:, :, :], 0.5, None, ALU.mult))

            def layer1():
                s_p["pe"].wait(v, 3)
                v.tensor_tensor(rb[:, 2, :], rb[:, 2, :], psY[:, 256:512], ALU.add)
                v.tensor_tensor(rb[:, 3, :], rb[:, 3, :], psT[1][:, 0:256], ALU.add)
                scaled(1)
                z.wait(v, 8)

            def film():
                y = s_p["film"]
                s_p["pe"].wait(v, 4)
                e_ = psT[0][:, 0:8 * B].rearrange("p (l o b) -> p l o b", l=2, o=4)
                pairs = [(l, d) for l in range(2) for d in range(2)]
                for l, d in pairs:
                    y.up(v.tensor_scalar(sc[:, l, d, :], e_[:, l, d, :], col[:, l, 8 + d:9 + d], 1.0, ALU.add,
                                         ALU.add))
                y.wait(v, 5)
                for l, d in pairs:
                    y.up(v.tensor_scalar(FA[:, l, d, :], sc[:, l, d, :], col[:, l, 12 + d:13 + d], 0.5, ALU.mult,
                                         ALU.mult))
                    y.up(v.scalar_tensor_tensor(FB[:, l, d, :], sc[:, l, d, :], col[:, l, 14 + d:15 + d],
                                                e_[:, l, 2 + d, :], ALU.mult, ALU.add))
                y.wait(v, 13)
                for l, d in pairs:
                    y.up(v.tensor_scalar(FB[:, l, d, :], FB[:, l, d, :], col[:, l, 10 + d:11 + d], 0.5, ALU.add,
                                         ALU.mult))
                loaded(v, 2)
                for k in range(4):
                    y.up(v.tensor_copy(BD[:, k, 128:136],
                                       diag[:, 0:128].rearrange("p (h e) -> p h e", e=DH)[:, :, 0]))
                y.wait(v, 21)

            def csplit(n, hf, late):
                r, b4 = HR[hf], 4 * hf
                if not late:
                    s_ct.wait(v, n, hf + 1)
                    s_cin[hf].wait(v, n - 1)
                    s_cs.up(v.tensor_copy(cp[hf][:, 0, :], psX[0:r, 0:128]))
                    s_cs.wait(v, n, b4 + 1)
                    s_cs.up(v.tensor_tensor(cr[0:r, :], psX[0:r, 0:128], cp[hf][:, 0, :], ALU.subtract))
                else:
                    s_cs.wait(v, n, b4 + 2)
                    s_cs.up(v.tensor_copy(cp[hf][:, 1, :], cr[0:r, :]))
                    s_cs.wait(v, n, b4 + 3)
                    s_cs.up(v.tensor_tensor(cp[hf][:, 2, :], cr[0:r, :], cp[hf][:, 1, :], ALU.subtract))

            def divide(n, k):
                s_yt.wait(v, n, k + 1)
                s_y.wait(v, n - 1, k + 1)
                ps = psX[:, :].rearrange("p (h d) -> p h d", d=32)
                s_yd.up(v.reciprocal(rd[:, :], ps[:, :, 16]))
                s_yd.wait(v, n, 4 * k + 1)
                s_yd.up(v.tensor_tensor(yr[:, k, :].rearrange("p (h d) -> p h d", d=DH), ps[:, :, 0:16],
                                        rd[:, :].rearrange("p (h a) -> p h a", a=1).to_broadcast([128, H, DH]),
                                        ALU.mult))

            def ystats(n, k):
                s_yd.wait(v, n, 4 * k + 2)
                s_yd.up(v.bn_stats(st[:, 2 + k, :], yr[:, k, :]))
                s_yd.wait(v, n, 4 * k + 3)
                s_yd.up(v.bn_aggr(mv[:, 2 + k, :], st[:, 2 + k, :]))

            def reduce(n, h):
                if ok(n):
                    s_sm.wait(v, n, h + 1)
                    s_ct.wait(v, n - 2)
                    s_mx.up(v.tensor_reduce(cm[n % 2][:, 2 * h:2 * h + 2],
                                            psM[h % 2][:, :].rearrange("p (k t) -> p k t", k=2),
                                            AX.X, ALU.max, negate=True))

            run = phase2_dve(v)

            def slot(t, i):
                if (t, i) == (1, 0):
                    silu()
                if (t, i) == (1, 4):
                    layer1()
                if (t, i) == (1, 7):
                    film()
                if i in (5, 7) and t < SV and ok(t):
                    split(v, t, (i - 5) // 2)
                if i == 2 and ok(t):
                    s_xT.wait(v, t)
                    s_vm.wait(v, t - 1)
                    s_xl.up(v.tensor_tensor(xT2[:, :, :].bitcast(F32R), psX[:, :].rearrange("p (k t) -> p k t", k=2),
                                            xT[:, :, :], ALU.subtract))
                reduce(t - 2, 2 * i)
                if i == 1 and ok(t - 3):
                    csplit(t - 3, 1, True)
                if i == 6 and ok(t - 2):
                    csplit(t - 2, 0, True)
                if i in (3, 4) and ok(t - 4):
                    ystats(t - 4, i - 3)
                if i == 0 and ok(t - 3):
                    csplit(t - 3, 1, False)
                if i == 5 and ok(t - 2):
                    csplit(t - 2, 0, False)
                if i in (2, 3) and ok(t - 4):
                    divide(t - 4, i - 2)
                if i == 7 and ok(t):
                    s_vm.wait(v, t)
                    s_v.wait(v, t - 1)
                    s_vt.up(v.tensor_tensor(vt[:, :, :], psX[:, :].rearrange("p (k d) -> p k d", k=2), vb0,
                                            ALU.add))
                reduce(t - 2, 2 * i + 1)
                if (t, i) == (B + 2, 3):
                    s_lo.wait(v, B - 1)
                    s_v.wait(v, B - 1)
                    parted(s_w1, W1[:, :, :, :], W1h, W1l)
                if i == 3 and ok(t + 1):
                    stats(t + 1)
            each(slot, run)
            late(run)

        @block.tensor
        def _(pe):
            loaded(pe, 0)
            done = s_p["pe"]
            s_p["mneg"].wait(pe, 1)
            for n, src in enumerate((mrow, keep)):
                for k in range(2):
                    c = 2 * B * n + B * k
                    ins = pe.transpose(psX[:, c:c + B], src[:, 128 * k:128 * k + 128], ident[0:B, 0:B])
            done.up(ins)

            def through(cols_of, rows_of):
                for n, l, w in cols_of:
                    for o in range(2):
                        for k in range(2):
                            pe.matmul(psM[0][:, 2 * n + o:2 * n + o + 1], W[l][w][:, k, 128 * o:128 * o + 128],
                                      col[:, l, 2 + k:3 + k], start=(k == 0), stop=(k == 1))
                for dst, l, w in rows_of:
                    for k in range(2):
                        ins = pe.matmul(dst, col[:, l, 2 + k:3 + k].to_broadcast([128, 128]), W[l][w][:, k, :],
                                        start=(k == 0), stop=(k == 1))
                done.up(ins)

            def embed(l):
                for o in range(4):
                    c = B * (4 * l + o)
                    for k in range(4):
                        ins = pe.matmul(psT[0][:, c:c + B], EW[:, l, k, 128 * o:128 * o + 128], cT[:, k, :],
                                        start=(k == 0), stop=(k == 3))
                return ins

            loaded(pe, 1)
            through(((0, 0, 0), (1, 0, 1)), ((psY[:, 0:256], 0, 2),))
            s_p["act"].wait(pe, 0)

            read = []

            def take(*by):
                if read:
                    read[0].wait(pe, *read[1:])
                read[:] = by

            def ctr(n, hf):
                s_mx.wait(pe, n, HB[hf + 1])
                s_ct.up(pe.transpose(psX[0:HR[hf], 0:128], cm[n % 2][:, 2 * HB[hf]:2 * HB[hf + 1]], ident[:, :]))

            run = phase2_pe(pe)

            def slot(t, i):
                if (t, i) == (0, 4):
                    s_p["act"].wait(pe, 1)
                    s_w0.wait(pe, 0)
                if (t, i) == (0, 7):
                    loaded(pe, 2)
                    for k in range(4):
                        ins = pe.transpose(psM[1][:, B * k:B * k + B], cond_sb[:, 128 * k:128 * k + 128],
                                           ident[0:B, 0:B])
                    done.up(ins)
                if (t, i) == (1, 2):
                    through(((2, 1, 1),), ((psY[:, 256:512], 1, 0), (psT[1][:, 0:256], 1, 2)))
                if (t, i) == (1, 5):
                    s_p["film"].wait(pe, 1)
                    embed(0)
                if (t, i) == (1, 6):
                    done.up(embed(1))
                if (t, i) == (2, 0):
                    s_p["act"].wait(pe, 3)
                if (t, i) == (3, 0):
                    s_p["ve0"].wait(pe, 8)
                    s_p["film"].wait(pe, 21)
                    s_p["pool"].wait(pe, 2)
                rowmax(t - 2, 2 * i)
                n = t - 3
                if ok(n):
                    G = 8 * n + i
                    if i == 0:
                        s_in.wait(pe, n)
                        s_cin[0].wait(pe, n)
                    if i == 5:
                        s_cin[1].wait(pe, n)
                    if G >= 2:
                        pe.wait_ge(s_ex.sem, G - 1)
                    for hh in range(2):
                        h = 2 * i + hh
                        for m in range(2):
                            ins = pe.matmul(psT[G % 2][:, 512 * hh + 256 * m:512 * hh + 256 * m + 256],
                                            Ks[n % 3][0:KS, h, 128 * m:128 * m + 128], Qs[n % 3][0:KS, h, :],
                                            start=True, stop=True)
                    s_sT.up(ins)
                if i in (7, 1):
                    rest(t, i)
                if i % 2:
                    n, gr = (t - 3, i // 2 - 1) if i > 1 else (t - 4, 3)
                    if ok(n):
                        s_ex.wait(pe, n, 2 * gr + 2)
                        s_v.wait(pe, n)
                        if 4 * n + gr:
                            pe.wait_ge(s_ye.sem, 4 * n + gr)
                        for m in range(2):
                            for j in range(4):
                                Pj = P[(8 * n + 2 * gr + j // 2) % 4]
                                c0 = 512 * (j % 2) + 256 * m
                                ins = pe.matmul(psY[32 * j:32 * j + 32, 0:T], Vp[n % 3][:, m, 4 * gr + j, :],
                                                Pj[:, c0:c0 + 256], start=(m == 0), stop=(m == 1))
                        s_pv.up(ins)
                if i not in (7, 1):
                    rest(t, i)
                rowmax(t - 2, 2 * i + 1)

            def rowmax(n, h):
                if ok(n):
                    if h == 0:
                        s_in.wait(pe, n)
                    if H * n + h >= 2:
                        pe.wait_ge(s_mx.sem, H * n + h - 1)
                    for k in range(2):
                        ins = pe.matmul(psM[h % 2][:, 256 * k:256 * k + 256],
                                        Qs[n % 3][0:KM, h, 128 * k:128 * k + 128], Ks[n % 3][0:KM, h, :],
                                        start=True, stop=True)
                    s_sm.up(ins)

            def rest(t, i):
                if i == 0 and ok(t - 3):
                    take(s_cs, t - 3, 6)
                    ctr(t - 3, 1)
                if i in (2, 3) and ok(t - 4):
                    n, k = t - 4, i - 2
                    s_ye.wait(pe, n)
                    take(s_yd, n, 4 * k + 2)
                    for q in range(4):
                        ins = pe.transpose(psX[:, 128 * q:128 * q + 128], yT[:, q, 128 * k:128 * k + 128], ident[:, :])
                    s_yt.up(ins)
                if i == 1 and ok(t):
                    s_xn.wait(pe, t)
                    take(s_xl, t, 1)
                    for d in range(2):
                        for k in range(2):
                            ins = pe.transpose(psX[:, 256 * d + 128 * k:256 * d + 128 * k + 128],
                                               xn[:, k, 128 * d:128 * d + 128], ident[:, :])
                    s_xtr.up(ins)
                if i in (4, 6) and ok(t):
                    w = (i - 4) // 2
                    s_xl.wait(pe, t)
                    take(s_qf, t, w + 1)
                    for o in range(2):
                        ins = product(pe, psX[:, 256 * o:256 * o + 256], cut((W0h[:, w, :, :], W0l[:, w, :, :]), o),
                                      cut((xT, xT2)))
                    s_qm.up(ins)
                if i == 5 and ok(t - 2):
                    take(s_cs, t - 2, 2)
                    ctr(t - 2, 0)
                if i == 7 and ok(t):
                    take(s_vt, t, 1)
                    for k in range(2):
                        ins = product(pe, psX[:, 256 * k:256 * k + 256], cut((xT, xT2), k),
                                      cut((W0h[:, 2, :, :], W0l[:, 2, :, :])))
                    s_vm.up(ins)
            each(slot, run)
            late(run)


def layer(inputs, l, names):
    return [inputs[f"L{l}_cond_{n}"] for n in names.split()]


def by_d(arrays):
    return [np.moveaxis(np.asarray(a).reshape(*a.shape[:-1], 8, 2, DH), -3, -1).reshape(a.shape) for a in arrays]


def packed(inputs):
    w = [by_d(layer(inputs, 0, "q_w k_w")) + layer(inputs, 0, "v_w out_w"), layer(inputs, 1, "Wq Wk Wv film_out_W")]
    w = np.stack([np.stack([np.asarray(a).reshape(2, 128, D) for a in ws]) for ws in w])
    e = np.stack([np.asarray(layer(inputs, 0, "emb_w")[0]), np.asarray(layer(inputs, 1, "film_emb_W")[0])])
    c = [layer(inputs, 0, "norm_w norm_b") + by_d(layer(inputs, 0, "q_b k_b"))
         + layer(inputs, 0, "emb_b sb_norm_w sb_norm_b"),
         layer(inputs, 1, "norm_scale norm_bias bq bk film_emb_b film_norm_scale film_norm_bias")]
    c = np.stack([np.concatenate([np.asarray(a).reshape(-1, 128) for a in cs]) for cs in c])
    r = np.stack([np.asarray(a) for a in layer(inputs, 0, "v_b out_b") + layer(inputs, 1, "bq bv film_out_b")])
    return {
        "weights": np.ascontiguousarray(w.transpose(3, 0, 1, 2, 4)),
        "emb": np.ascontiguousarray(e.reshape(2, 4, 128, 2 * D).transpose(2, 0, 1, 3)),
        "cols": np.ascontiguousarray(c.transpose(2, 0, 1)),
        "rows": r,
        "ident": np.eye(128, dtype=np.float32),
        "diag": np.kron(np.eye(128 // DH, dtype=np.float32), np.ones((DH, DH), np.float32)),
    }


def kernel(**inputs):
    import concourse.bacc as bacc
    from concourse.bass_utils import run_bass_kernel_spmd

    nc = bacc.Bacc("TRN2", target_bir_lowering=False, num_devices=1)
    given = {
        "x": inputs["x"], "cond": inputs["cond_2048"], "mask_f": inputs["mask_BxS_ff1"],
        "mask_i": inputs["mask_BxS_ik0"],
    }
    arrays, args = {}, []
    for name, a in (given | packed(inputs)).items():
        a = np.ascontiguousarray(a)
        arrays[f"in_{name}"] = a
        args.append(nc.dram_tensor(f"in_{name}", a.shape, mybir.dt.from_np(a.dtype), kind="ExternalInput").ap())
    args.append(nc.dram_tensor("out_0", (B, T, D), F32, kind="ExternalOutput").ap())
    bass_cond_seq_kernel(nc, *args)
    r = run_bass_kernel_spmd(nc, [arrays], core_ids=[0])
    return r.results[0]["out_0"]
```
